# Optimizing a Trainium2 kernel written in Bass

```python
import numpy as np
import jax
import jax.numpy as jnp

def _softmax(x, axis=-1):
    return jax.nn.softmax(x, axis=axis)

def _gelu(x):
    return jax.nn.gelu(x, approximate=True)

def _silu(x):
    return jax.nn.silu(x)

def _sigmoid(x):
    return jax.nn.sigmoid(x)

def _layernorm(x, axis=-1, eps=1e-05):
    m = jnp.mean(x, axis=axis, keepdims=True)
    v = jnp.var(x, axis=axis, keepdims=True)
    return (x - m) / jnp.sqrt(v + eps)

def _scatter_add(tgt, idx, src, axis=0):
    return tgt.at[idx].add(src)

def _segment_sum(src, seg, n):
    return jax.ops.segment_sum(src, seg, n)
kernel_name = 'mk_xattn_ffn_d1_seqx_r8_c25023'

def setup_inputs(seed: int=0):
    np.random.seed(seed)
    _w = jnp.asarray

    def _rec_inputs():
        import jax
        import jax.numpy as jnp
        _rk = jax.random.key(seed)
        x = -7.109e-05 + 0.9999 * jax.random.normal(jax.random.fold_in(_rk, 1), (32, 56, 512), jnp.float32)
        _lenS = 56 - jax.random.randint(jax.random.fold_in(_rk, 7), (32,), 0, max(1, 56 // 4) + 1, jnp.int32)
        _lenS2 = 1500 - jax.random.randint(jax.random.fold_in(_rk, 8), (32,), 0, max(1, 1500 // 4) + 1, jnp.int32)
        _ctx_4096P = jax.random.normal(jax.random.fold_in(_rk, 11), (32, 16, 512), jnp.float32)
        _ctx_4096c = jax.random.dirichlet(jax.random.fold_in(_rk, 511), 0.3 * jnp.ones((16,), jnp.float32), (32, 1500))
        _ctx_4096t = jnp.einsum('bsk,bkd->bsd', _ctx_4096c, _ctx_4096P)
        _ctx_4096t = _ctx_4096t * jax.lax.rsqrt(jnp.mean(jnp.square(_ctx_4096t)) + 1e-12) * 0.953939
        ctx_4096 = -2.6191e-05 + 0.999952 * (_ctx_4096t + 0.3 * jax.random.normal(jax.random.fold_in(_rk, 611), (32, 1500, 512), jnp.float32))
        return (x, ctx_4096)
    x, ctx_4096 = _rec_inputs()

    def _L0_xattn_setup():
        import jax, jax.numpy as jnp
        import numpy as np
        TEXT_DIM = 512
        FEATURE_DIM = 512

        def _xavier_uniform(key, shape):
            fan_in, fan_out = (shape[1], shape[0])
            limit = float(np.sqrt(6.0 / (fan_in + fan_out)))
            return jax.random.uniform(key, shape, jnp.float32, -limit, limit)
        key = jax.random.key(seed)
        k1, k2, k3, k4 = jax.random.split(key, 4)
        text = jax.random.normal(k1, (8, 256, TEXT_DIM), jnp.float32)
        features = jax.random.normal(k2, (8, 72, FEATURE_DIM), jnp.float32)
        Wq = _xavier_uniform(k3, (FEATURE_DIM, TEXT_DIM))
        bq = jnp.zeros((FEATURE_DIM,), jnp.float32)
        Wk = _xavier_uniform(k4, (FEATURE_DIM, FEATURE_DIM))
        bk = jnp.zeros((FEATURE_DIM,), jnp.float32)
        return {'text': text, 'features': features, 'Wq': Wq, 'bq': bq, 'Wk': Wk, 'bk': bk}
    _L0_xattn_all = _L0_xattn_setup()
    _L0_xattn_in = {k: v for k, v in _L0_xattn_all.items() if k in ('Wq', 'bq', 'Wk', 'bk')}
    del _L0_xattn_all

    def _L0_ffn_setup():
        import jax, jax.numpy as jnp
        import numpy as np
        D_IN, D_OUT = (512, 512)
        B, S = (2, 256)
        key = jax.random.key(seed)
        kx, kw = jax.random.split(key)
        x = jax.random.normal(kx, (B, S, D_IN), dtype=jnp.float32)
        w = jax.random.normal(kw, (D_IN, D_OUT), dtype=jnp.float32)
        sign = jnp.where(w >= 0, 1.0, -1.0).astype(jnp.float32)
        scale = jnp.abs(w).mean().astype(jnp.float32)
        return {'x': x, 'sign': sign, 'scale': scale}
    _L0_ffn_all = _L0_ffn_setup()
    _L0_ffn_in = {k: v for k, v in _L0_ffn_all.items() if k in ('sign', 'scale')}
    del _L0_ffn_all
    return {'x': x, 'ctx_4096': ctx_4096, 'L0_xattn_Wq': _L0_xattn_in['Wq'], 'L0_xattn_bq': _L0_xattn_in['bq'], 'L0_xattn_Wk': _L0_xattn_in['Wk'], 'L0_xattn_bk': _L0_xattn_in['bk'], 'L0_ffn_sign': _L0_ffn_in['sign'], 'L0_ffn_scale': _L0_ffn_in['scale']}

def reference(x, ctx_4096, L0_xattn_Wq, L0_xattn_bq, L0_xattn_Wk, L0_xattn_bk, L0_ffn_sign, L0_ffn_scale):
    import jax
    import jax.numpy as jnp

    def _L0_xattn_ref(text, features, Wq, bq, Wk, bk):
        import jax, jax.numpy as jnp
        import numpy as np
        TEXT_DIM = 512
        FEATURE_DIM = 512

        def _xavier_uniform(key, shape):
            fan_in, fan_out = (shape[1], shape[0])
            limit = float(np.sqrt(6.0 / (fan_in + fan_out)))
            return jax.random.uniform(key, shape, jnp.float32, -limit, limit)
        Q = jnp.einsum('btx,dx->btd', text, Wq) + bq
        K = jnp.einsum('bpx,dx->bpd', features, Wk) + bk
        scale = 1.0 / jnp.sqrt(jnp.asarray(K.shape[-1], K.dtype))
        scores = jnp.einsum('btd,bpd->btp', Q, K) * scale
        attn = jax.nn.softmax(scores, axis=-1)
        attended = jnp.einsum('btp,bpd->btd', attn, features)
        return attended

    def _L0_ffn_ref(x, sign, scale):
        import jax, jax.numpy as jnp
        import numpy as np
        D_IN, D_OUT = (512, 512)
        B, S = (2, 256)
        s = jax.nn.softplus(scale)
        return jnp.einsum('bsi,io->bso', x, sign) * s
    x = x + _L0_xattn_ref(_layernorm(x, axis=-1), ctx_4096, L0_xattn_Wq, L0_xattn_bq, L0_xattn_Wk, L0_xattn_bk)
    x = x + _L0_ffn_ref(_layernorm(x, axis=-1), L0_ffn_sign, L0_ffn_scale)
    return x

_drawn_inputs = setup_inputs


def setup_inputs(seed=0):
    import zlib

    import numpy as np

    out = dict(_drawn_inputs(seed))
    spreads = {'L0_xattn_bq': (0.0, 0.466), 'L0_xattn_bk': (0.0, 0.8)}
    factors = {}
    for name, (base, spread) in spreads.items():
        noise = np.random.default_rng([zlib.crc32(name.encode()), seed]).standard_normal(out[name].shape)
        drawn = base * np.exp(spread * noise) if base else spread * noise
        out[name] = jnp.asarray(drawn.astype(out[name].dtype))
    for name, factor in factors.items():
        out[name] = (out[name] * factor).astype(out[name].dtype)
    return out
```

```python
from contextlib import ExitStack

import concourse.bass as bass
from concourse import mybir

F32 = mybir.dt.float32
ALU = mybir.AluOpType
ACT = mybir.ActivationFunctionType
AX_X = mybir.AxisListType.X

HALF = 64
GROUPS = 3
RING = 3

KT = [("dve", "act")[i % 2] for i in range(8)]
XT_USE = [("xT", 0, "act")]
T_USES = [[("kT%d" % g, i, KT[i]) for i in range(8)] for g in range(GROUPS)]
Q_USE = [("q", 0, "dve")]
PT_USES = [("pT", 0, "act"), ("pT", 1, "dve"), ("pT", 2, "act")]
YT_USE = [("yT", 0, "act")]
FIRST = XT_USE + T_USES[0] + Q_USE + T_USES[1] + T_USES[2]
STEADY = XT_USE + T_USES[0] + Q_USE + PT_USES + T_USES[1] + T_USES[2] + YT_USE
TAIL = PT_USES + YT_USE


def ring_position(steps, p, what, index):
    if isinstance(p, int) and p == 0:
        uses, before, done = FIRST, 0, {"act": 0, "dve": 0}
    else:
        uses = TAIL if isinstance(p, int) and p == steps else STEADY
        before = (p - 1) * len(STEADY) + len(FIRST)
        done = {e: (p - 1) * sum(u[2] == e for u in STEADY) + sum(u[2] == e for u in FIRST)
                for e in ("act", "dve")}
    at = [u[:2] for u in uses].index((what, index))
    engine = uses[at][2]
    base = 0 if isinstance(p, int) and p == 0 else len(FIRST)
    bank = (base + at) % RING
    return bank, before + at, done[engine] + sum(u[2] == engine for u in uses[:at]), engine


def ring_previous(steps, p, what, index):
    uses = FIRST if isinstance(p, int) and p == 0 else TAIL if isinstance(p, int) and p == steps else STEADY
    at = [u[:2] for u in uses].index((what, index))
    if at < RING:
        return None
    _, _, n, engine = ring_position(steps, p, *uses[at - RING][:2])
    return engine, n + 1


def xattn_ffn_kernel(nc, x, ctx_in, Wq, bq, Wk, bk, sign, scale, out):
    B, T, D = x.shape
    S = ctx_in.shape[1]
    STEPS = B // 2
    C = D // 128
    KT_N = 12
    Q = S // KT_N
    KPG = KT_N // GROUPS
    GK = KPG * Q
    R = HALF + T
    SCALE = float(D) ** -0.5
    EPS = 1e-5
    MAIN = Q // 16 * 16
    assert Q * KT_N == S and Q <= 128 and GK <= 512 and T <= HALF and STEPS % 2 == 0

    x_v = x.rearrange("(n b) t d -> n b t d", b=2)
    out_v = out.rearrange("(n b) t d -> n b t d", b=2)
    ctx_v = ctx_in.rearrange("(n b) (q k) d -> n q b (k d)", b=2, k=KT_N)

    with ExitStack() as stack:
        def sb(name, shape):
            return stack.enter_context(nc.sbuf_tensor(name, shape, F32))

        def pb(name, shape):
            return stack.enter_context(nc.psum_tensor(name, shape, F32))

        def sem(name):
            return stack.enter_context(nc.semaphore(name))

        keys = [sb(f"keys{i}", [128, 2, KT_N, D]) for i in range(2)]
        keysT = [sb(f"keysT{i}", [128, 2, C, GK]) for i in range(2)]
        wq = sb("wq", [128, C, D])
        wk = sb("wk", [128, C, D])
        bqc = sb("bqc", [128, C])
        bkc = sb("bkc", [128, C])
        bprod = sb("bprod", [128, C])
        bsum = sb("bsum", [128, 1])
        wqk = sb("wqk", [128, C, D])
        qbias = sb("qbias", [128, C])
        cvec = sb("cvec", [128, C])
        cconst = sb("cconst", [128, 1])
        signs = sb("signs", [128, C, D])
        gain_in = sb("gain_in", [1, 1])
        gain = sb("gain", [128, 1])
        gabs = sb("gabs", [128, 1])
        gexp = sb("gexp", [128, 1])
        glog = sb("glog", [128, 1])
        softplus = sb("softplus", [128, 1])
        ones = sb("ones", [128, 128])
        ident = sb("ident", [128, 128])
        minus_half = sb("minus_half", [128, 1])
        eps = sb("eps", [128, 1])
        xs = [sb(f"xs{i}", [128, D]) for i in range(2)]
        xn = sb("xn", [128, D])
        xnT = sb("xnT", [128, C, 2 * HALF])
        qT = sb("qT", [128, C, 2, T])
        crow = sb("crow", [128, 1])
        gmax = sb("gmax", [128, GROUPS])
        smax = sb("smax", [128, 1])
        cmax = sb("cmax", [128, 1])
        ebias = sb("ebias", [128, 1])
        probs = sb("probs", [128, KT_N, Q])
        gsum = sb("gsum", [128, GROUPS])
        rsum = sb("rsum", [128, 1])
        rinv = sb("rinv", [128, 1])
        probsT = sb("probsT", [128, KT_N, R])
        x1 = sb("x1", [128, D])
        x1n = sb("x1n", [128, D])
        x1nT = sb("x1nT", [128, C, R])
        result = sb("result", [128, D])
        xstat = sb("xstat", [128, 6])
        xmv = sb("xmv", [128, 2])
        xvar = sb("xvar", [128, 1])
        xrstd = sb("xrstd", [128, 1])
        ystat = sb("ystat", [128, 6])
        ymv = sb("ymv", [128, 2])
        yvar = sb("yvar", [128, 1])
        yrstd = sb("yrstd", [128, 1])

        scores = pb("scores", [128, GROUPS, 512])
        ring = [pb(f"ring{i}", [128, 512]) for i in range(RING)]
        attended = pb("attended", [128, 512])
        ffn = pb("ffn", [128, 512])

        w_loaded = sem("w_loaded")
        b_loaded = sem("b_loaded")
        sign_loaded = sem("sign_loaded")
        gain_loaded = sem("gain_loaded")
        keys_loaded = [[sem(f"keys_loaded{i}_{g}") for g in range(GROUPS)] for i in range(2)]
        x_loaded = [sem(f"x_loaded{i}") for i in range(2)]
        out_stored = sem("out_stored")
        consts_ready = sem("consts_ready")
        ident_zero = sem("ident_zero")
        x_zeroed = sem("x_zeroed")
        bprod_ready = sem("bprod_ready")
        bsum_ready = sem("bsum_ready")
        setup_small = sem("setup_small")
        setup_mm = sem("setup_mm")
        setup_act = sem("setup_act")
        setup_dve = sem("setup_dve")
        psum_zeroed = sem("psum_zeroed")
        gain_copied = sem("gain_copied")
        gabs_ready = sem("gabs_ready")
        gexp_ready = sem("gexp_ready")
        glog_ready = sem("glog_ready")
        softplus_ready = sem("softplus_ready")
        ring_full = sem("ring_full")
        ring_act = sem("ring_act")
        ring_dve = sem("ring_dve")
        xstat_ready = sem("xstat_ready")
        xmv_ready = sem("xmv_ready")
        xvar_ready = sem("xvar_ready")
        xrstd_ready = sem("xrstd_ready")
        xn_ready = sem("xn_ready")
        ystat_ready = sem("ystat_ready")
        ymv_ready = sem("ymv_ready")
        yvar_ready = sem("yvar_ready")
        yrstd_ready = sem("yrstd_ready")
        x1_ready = sem("x1_ready")
        x1n_ready = sem("x1n_ready")
        crow_ready = sem("crow_ready")
        scores_ready = sem("scores_ready")
        gmax_ready = sem("gmax_ready")
        smax_ready = sem("smax_ready")
        cmax_ready = sem("cmax_ready")
        ebias_ready = sem("ebias_ready")
        exp_ready = sem("exp_ready")
        rsum_ready = sem("rsum_ready")
        rinv_ready = sem("rinv_ready")
        keys_used = sem("keys_used")
        attended_ready = sem("attended_ready")
        ffn_ready = sem("ffn_ready")
        result_ready = sem("result_ready")

        ring_sem = {"act": ring_act, "dve": ring_dve}

        block = stack.enter_context(nc.Block())

        def over_steps(engine, step):
            step(0, 0, 0)
            with engine.Fori(0, STEPS // 2 - 1) as i:
                step(i * 2 + 1, 1, i)
                step(i * 2 + 2, 0, i + 1)
            step(STEPS - 1, 1, STEPS // 2 - 1)

        @block.sync
        def _(sp):
            def load_keys(p, par, g):
                cols = slice(g * KPG * D, (g + 1) * KPG * D)
                dst = keys[par][:, :, :, :].rearrange("q b k d -> q b (k d)")
                src = ctx_v[bass.ds(p, 1)].rearrange("n q b e -> (n q) b e")
                for a, z in ((0, MAIN), (MAIN, Q)):
                    sp.dma_start(dst[a:z, :, cols], src[a:z, :, cols]).then_inc(keys_loaded[par][g], 16)

            def load_x(p, par):
                src = x_v[bass.ds(p, 1)].rearrange("n b t d -> (n b) t d")
                for b in range(2):
                    sp.dma_start(xs[par][b * HALF:b * HALF + T, :], src[b]).then_inc(x_loaded[par], 16)

            def store(p):
                dst = out_v[bass.ds(p, 1)].rearrange("n b t d -> (n b) t d")
                for b in range(2):
                    sp.dma_start(dst[b], result[b * HALF:b * HALF + T, :]).then_inc(out_stored, 16)

            sp.dma_start(wq[:], Wq.rearrange("(p c) x -> p c x", c=C)).then_inc(w_loaded, 16)
            sp.dma_start(wk[:], Wk.rearrange("(p c) x -> p c x", c=C)).then_inc(w_loaded, 16)
            sp.dma_start(bqc[:], bq.rearrange("(p c) -> p c", c=C)).then_inc(b_loaded, 16)
            sp.dma_start(bkc[:], bk.rearrange("(p c) -> p c", c=C)).then_inc(b_loaded, 16)
            sp.dma_start(gain_in[:], scale.rearrange("(a b) -> a b", a=1)).then_inc(gain_loaded, 16)
            sp.wait_ge(x_zeroed, 2)
            load_x(0, 0)
            for g in range(GROUPS):
                load_keys(0, 0, g)
            load_x(1, 1)
            sp.dma_start(signs[:], sign.rearrange("(c p) o -> p c o", p=128)).then_inc(sign_loaded, 16)
            for g in range(GROUPS):
                load_keys(1, 1, g)

            def step(p, par, last=False):
                if not last:
                    for g in range(GROUPS):
                        if g < GROUPS - 1:
                            sp.wait_ge(keys_used, (p - 1) * (GROUPS - 1) + g + 1)
                        else:
                            sp.wait_ge(attended_ready, p)
                        load_keys(p + 1, 1 - par, g)
                    sp.wait_ge(x1_ready, p)
                    load_x(p + 1, 1 - par)
                sp.wait_ge(result_ready, p)
                store(p - 1)

            with sp.Fori(0, STEPS // 2 - 1) as i:
                step(i * 2 + 1, 1)
                step(i * 2 + 2, 0)
            step(STEPS - 1, 1, last=True)
            sp.wait_ge(result_ready, STEPS)
            store(STEPS - 1)
            sp.wait_ge(out_stored, 32 * STEPS)

        @block.gpsimd
        def _(pool):
            nc.gpsimd.memset(xs[0][:], 0.0).then_inc(x_zeroed, 1)
            nc.gpsimd.memset(xs[1][:], 0.0).then_inc(x_zeroed, 1)
            nc.gpsimd.memset(ident[:], 0.0).then_inc(ident_zero, 1)
            nc.gpsimd.memset(ones[:], 1.0).then_inc(consts_ready, 1)
            nc.gpsimd.memset(minus_half[:], -0.5).then_inc(consts_ready, 1)
            nc.gpsimd.memset(eps[:], EPS).then_inc(consts_ready, 1)
            pool.wait_ge(ident_zero, 1)
            nc.gpsimd.affine_select(out=ident[:], in_=ident[:], compare_op=ALU.not_equal, fill=1.0, base=0,
                                    pattern=[[-1, 128]], channel_multiplier=1).then_inc(consts_ready, 1)
            pool.wait_ge(consts_ready, 3)

            def x_rstd(p):
                pool.wait_ge(xmv_ready, p + 1)
                nc.gpsimd.tensor_tensor(xvar[0:R, :], xmv[0:R, 1:2], eps[0:R, :], ALU.add).then_inc(xvar_ready, 1)
                pool.wait_ge(xvar_ready, p + 1)
                nc.gpsimd.tensor_tensor(xrstd[0:R, :], xvar[0:R, :], minus_half[0:R, :],
                                        ALU.pow).then_inc(xrstd_ready, 1)

            def y_rstd(p):
                pool.wait_ge(ymv_ready, p + 1)
                nc.gpsimd.tensor_tensor(yvar[0:R, :], ymv[0:R, 1:2], eps[0:R, :], ALU.add).then_inc(yvar_ready, 1)
                pool.wait_ge(yvar_ready, p + 1)
                nc.gpsimd.tensor_tensor(yrstd[0:R, :], yvar[0:R, :], minus_half[0:R, :],
                                        ALU.pow).then_inc(yrstd_ready, 1)

            x_rstd(0)
            x_rstd(1)
            with pool.Fori(1, STEPS - 1) as p:
                y_rstd(p - 1)
                x_rstd(p + 1)
            y_rstd(STEPS - 2)
            y_rstd(STEPS - 1)

        def setup_bank(xc):
            return scores[:, xc, :] if xc < GROUPS else attended[:, :]

        def ring_take(engine, p, what, index):
            bank, n, _, _ = ring_position(STEPS, p, what, index)
            engine.wait_ge(ring_full, n + 1)
            return ring[bank]

        @block.scalar
        def _(act):
            def copy(out_ap, in_ap):
                return nc.scalar.activation(out_ap, in_ap, ACT.Copy)

            def keys_evac(p, g, i):
                if KT[i] == "act":
                    bank = ring_take(act, p, "kT%d" % g, i)
                    copy(kT_dst(p, g, i), bank[:, 0:GK]).then_inc(ring_act, 1)

            def x_evac(p):
                bank = ring_take(act, p, "xT", 0)
                copy(xnT[:, :, 0:R], bank[:, 0:C * R].rearrange("p (c r) -> p c r", c=C)).then_inc(ring_act, 1)

            def exps(p, g):
                if g == 0:
                    act.wait_ge(ebias_ready, p + 1)
                nc.scalar.activation(probs[0:R, KPG * g:KPG * (g + 1), :],
                                     scores[0:R, g, 0:GK].rearrange("r (k q) -> r k q", q=Q), ACT.Exp,
                                     bias=ebias[0:R, :], scale=1.0,
                                     accum_out=gsum[0:R, g:g + 1]).then_inc(exp_ready, 1)

            def probs_evac(p, g):
                bank = ring_take(act, p + 1, "pT", g)
                copy(probsT[0:Q, KPG * g:KPG * (g + 1), :],
                     bank[0:Q, 0:KPG * R].rearrange("q (k r) -> q k r", r=R)).then_inc(ring_act, 1)

            act.wait_ge(gabs_ready, 1)
            nc.scalar.activation(gexp[:], gabs[:], ACT.Exp, scale=-1.0).then_inc(gexp_ready, 1)
            act.wait_ge(gexp_ready, 1)
            nc.scalar.activation(glog[:], gexp[:], ACT.Ln, bias=1.0).then_inc(glog_ready, 1)
            for xc in (0, 2):
                act.wait_ge(setup_mm, xc + 1)
                nc.scalar.activation(wqk[:, xc, :], setup_bank(xc), ACT.Copy, scale=SCALE).then_inc(setup_act, 1)

            def step(p, par, half):
                x_evac(p)
                first = isinstance(p, int) and p == 0
                for i in range(8):
                    keys_evac(p, 0, i)
                    if not first and i in (1, 3, 5):
                        exps(p - 1, i // 2)
                if not first:
                    probs_evac(p - 1, 0)
                    probs_evac(p - 1, 2)
                for g in (1, 2):
                    for i in range(8):
                        keys_evac(p, g, i)
                if not first:
                    y_evac(p - 1)

            def y_evac(p):
                bank = ring_take(act, p + 1, "yT", 0)
                copy(x1nT[:, :, :], bank[:, 0:C * R].rearrange("p (c r) -> p c r", c=C)).then_inc(ring_act, 1)

            def kT_dst(p, g, i):
                return keysT[(kT_par[0] + g) % 2][:, i % 2, i // 2, :]

            kT_par = [0]

            def step_par(p, par, half):
                kT_par[0] = par
                step(p, par, half)

            over_steps(act, step_par)
            for g in range(GROUPS):
                exps(STEPS - 1, g)
            probs_evac(STEPS - 1, 0)
            probs_evac(STEPS - 1, 2)
            y_evac(STEPS - 1)

        @block.vector
        def _(dve):
            def keys_evac(p, par, g, i):
                if KT[i] == "dve":
                    bank = ring_take(dve, p, "kT%d" % g, i)
                    nc.vector.tensor_copy(keysT[(par + g) % 2][:, i % 2, i // 2, :],
                                          bank[:, 0:GK]).then_inc(ring_dve, 1)

            def group_max(p, g):
                dve.wait_ge(scores_ready, p * GROUPS + g + 1)
                nc.vector.reduce_max(gmax[0:R, g:g + 1], scores[0:R, g, 0:GK], AX_X).then_inc(gmax_ready, 1)

            def softmax_bias(p):
                dve.wait_ge(gmax_ready, (p + 1) * GROUPS)
                nc.vector.reduce_max(smax[0:R, :], gmax[0:R, :], AX_X).then_inc(smax_ready, 1)
                dve.wait_ge(smax_ready, p + 1)
                dve.wait_ge(crow_ready, p + 1)
                nc.vector.tensor_tensor(cmax[0:R, :], smax[0:R, :], crow[0:R, :], ALU.add).then_inc(cmax_ready, 1)
                dve.wait_ge(cmax_ready, p + 1)
                nc.vector.tensor_tensor(ebias[0:R, :], crow[0:R, :], cmax[0:R, :],
                                        ALU.subtract).then_inc(ebias_ready, 1)

            def x_stats(p, par, half):
                dve.wait_ge(x_loaded[par], half * 32 + 32)
                nc.vector.bn_stats(xstat[0:R, :], xs[par][0:R, :]).then_inc(xstat_ready, 1)

            def x_aggregate(p):
                nc.vector.bn_aggr(xmv[0:R, :], xstat[0:R, :]).then_inc(xmv_ready, 1)

            def x_normalise(p, par):
                dve.wait_ge(xrstd_ready, p + 1)
                if not (isinstance(p, int) and p == 0):
                    dve.wait_ge(ring_full, ring_position(STEPS, p - 1, "xT", 0)[1] + 1)
                nc.vector.tensor_scalar(xn[0:R, :], xs[par][0:R, :], xmv[0:R, 0:1], xrstd[0:R, :],
                                        ALU.subtract, ALU.mult).then_inc(xn_ready, 1)

            def q_evac(p):
                bank = ring_take(dve, p, "q", 0)
                nc.vector.tensor_tensor(crow[0:R, :], bank[0:R, C * 2 * T:C * 2 * T + 1], cconst[0:R, :],
                                        ALU.add).then_inc(crow_ready, 1)
                nc.vector.tensor_tensor(qT[:, :, :, :].rearrange("p c b t -> p c (b t)"),
                                        bank[:, 0:C * 2 * T].rearrange("p (c n) -> p c n", c=C),
                                        qbias[:, :].rearrange("p (c o) -> p c o", o=1).to_broadcast([128, C, 2 * T]),
                                        ALU.add).then_inc(ring_dve, 1)

            def row_sums(p):
                dve.wait_ge(exp_ready, (p + 1) * GROUPS)
                nc.vector.reduce_sum(rsum[0:R, :], gsum[0:R, :], AX_X).then_inc(rsum_ready, 1)
                dve.wait_ge(rsum_ready, p + 1)
                nc.vector.reciprocal(rinv[0:R, :], rsum[0:R, :]).then_inc(rinv_ready, 1)

            def probs_evac(p, g):
                bank = ring_take(dve, p + 1, "pT", g)
                nc.vector.tensor_copy(probsT[0:Q, KPG * g:KPG * (g + 1), :],
                                      bank[0:Q, 0:KPG * R].rearrange("q (k r) -> q k r", r=R)).then_inc(ring_dve, 1)

            def residual(p, par):
                dve.wait_ge(attended_ready, p + 1)
                dve.wait_ge(rinv_ready, p + 1)
                nc.vector.scalar_tensor_tensor(out=x1[0:R, :], in0=attended[0:R, :], scalar=rinv[0:R, :],
                                               in1=xs[par][0:R, :], op0=ALU.mult, op1=ALU.add).then_inc(x1_ready, 1)

            def x1_stats(p):
                dve.wait_ge(x1_ready, p + 1)
                nc.vector.bn_stats(ystat[0:R, :], x1[0:R, :]).then_inc(ystat_ready, 1)

            def x1_aggregate(p):
                nc.vector.bn_aggr(ymv[0:R, :], ystat[0:R, :]).then_inc(ymv_ready, 1)

            def x1_normalise(p):
                dve.wait_ge(yrstd_ready, p + 1)
                nc.vector.tensor_scalar(x1n[0:R, :], x1[0:R, :], ymv[0:R, 0:1], yrstd[0:R, :],
                                        ALU.subtract, ALU.mult).then_inc(x1n_ready, 1)

            def finish(p):
                dve.wait_ge(ffn_ready, p + 1)
                if not (isinstance(p, int) and p == 0):
                    dve.wait_ge(out_stored, p * 32)
                nc.vector.scalar_tensor_tensor(out=result[0:R, :], in0=ffn[0:R, :], scalar=softplus[0:R, :],
                                               in1=x1[0:R, :], op0=ALU.mult, op1=ALU.add).then_inc(result_ready, 1)

            dve.wait_ge(b_loaded, 32)
            nc.vector.tensor_tensor(bprod[:], bqc[:], bkc[:], ALU.mult).then_inc(bprod_ready, 1)
            dve.wait_ge(bprod_ready, 1)
            nc.vector.reduce_sum(bsum[:], bprod[:], AX_X).then_inc(bsum_ready, 1)
            dve.wait_ge(setup_small, 1)
            nc.vector.tensor_scalar(qbias[:], ffn[:, 0:C], SCALE, None, ALU.mult).then_inc(setup_dve, 1)
            nc.vector.tensor_scalar(cvec[:], ffn[:, C:2 * C], SCALE, None, ALU.mult).then_inc(setup_dve, 1)
            nc.vector.tensor_scalar(cconst[:], ffn[:, 2 * C:2 * C + 1], SCALE, None, ALU.mult).then_inc(setup_dve, 1)
            nc.vector.tensor_copy(gain[:], ffn[:, 2 * C + 1:2 * C + 2]).then_inc(gain_copied, 1)
            dve.wait_ge(gain_copied, 1)
            nc.vector.scalar_tensor_tensor(out=gabs[:], in0=gain[:], scalar=-1.0, in1=gain[:],
                                           op0=ALU.mult, op1=ALU.max).then_inc(gabs_ready, 1)
            x_stats(0, 0, 0)
            dve.wait_ge(xstat_ready, 1)
            x_aggregate(0)
            x_normalise(0, 0)
            for xc in (1, 3):
                dve.wait_ge(setup_mm, xc + 1)
                nc.vector.tensor_scalar(wqk[:, xc, :], setup_bank(xc), SCALE, None, ALU.mult).then_inc(setup_dve, 1)
            dve.wait_ge(glog_ready, 1)
            nc.vector.scalar_tensor_tensor(out=softplus[:], in0=gain[:], scalar=0.0, in1=glog[:],
                                           op0=ALU.max, op1=ALU.add).then_inc(softplus_ready, 1)
            dve.wait_ge(setup_dve, 5)
            dve.wait_ge(setup_act, 2)
            nc.vector.memset(scores[:, :, :], 0.0).then_inc(psum_zeroed, 1)
            nc.vector.memset(attended[:, :], 0.0).then_inc(psum_zeroed, 1)
            dve.wait_ge(softplus_ready, 1)
            dve.wait_ge(psum_zeroed, 2)

            def step(p, par, half, last=False):
                first = isinstance(p, int) and p == 0
                if not first:
                    group_max(p - 1, 2)
                    softmax_bias(p - 1)
                for i in range(8):
                    keys_evac(p, par, 0, i)
                q_evac(p)
                if not first:
                    row_sums(p - 1)
                    probs_evac(p - 1, 1)
                for i in range(8):
                    keys_evac(p, par, 1, i)
                    if not first and i == 1:
                        residual(p - 1, 1 - par)
                    if not first and i == 3:
                        x1_stats(p - 1)
                        dve.wait_ge(ystat_ready, p)
                    if not first and i == 5:
                        x1_aggregate(p - 1)
                group_max(p, 0)
                if not first:
                    x1_normalise(p - 1)
                for i in range(8):
                    keys_evac(p, par, 2, i)
                if not last:
                    x_stats(p + 1, 1 - par, half if par == 0 else half + 1)
                if not last:
                    dve.wait_ge(xstat_ready, p + 2)
                group_max(p, 1)
                if not last:
                    x_aggregate(p + 1)
                    x_normalise(p + 1, 1 - par)
                if not first:
                    finish(p - 1)

            step(0, 0, 0)
            with dve.Fori(0, STEPS // 2 - 1) as i:
                step(i * 2 + 1, 1, i)
                step(i * 2 + 2, 0, i + 1)
            step(STEPS - 1, 1, STEPS // 2 - 1, last=True)
            p = STEPS - 1
            group_max(p, 2)
            softmax_bias(p)
            row_sums(p)
            probs_evac(p, 1)
            residual(p, 1)
            x1_stats(p)
            dve.wait_ge(ystat_ready, p + 1)
            x1_aggregate(p)
            x1_normalise(p)
            finish(p)

        @block.tensor
        def _(pe):
            def ring_bank(p, what, index):
                previous = ring_previous(STEPS, p, what, index)
                if previous:
                    pe.wait_ge(ring_sem[previous[0]], previous[1])
                return ring[ring_position(STEPS, p, what, index)[0]]

            def evacuated(p, what, index):
                _, _, n, engine = ring_position(STEPS, p, what, index)
                pe.wait_ge(ring_sem[engine], n + 1)

            def transpose_x(p, src, ready, what):
                pe.wait_ge(ready[0], ready[1])
                bank = ring_bank(p, what, 0)
                for c in range(C):
                    mm = pe.transpose(bank[:, c * R:(c + 1) * R], src[0:R, c * 128:(c + 1) * 128], ident[0:R, 0:R])
                mm.then_inc(ring_full, 1)

            def transpose_keys(p, par, half, g):
                pe.wait_ge(keys_loaded[par][g], half * 32 + 32)
                for i in range(8):
                    b, c = i % 2, i // 2
                    bank = ring_bank(p, "kT%d" % g, i)
                    for k in range(KPG):
                        mm = pe.transpose(bank[:, k * Q:(k + 1) * Q],
                                          keys[par][0:Q, b, KPG * g + k, c * 128:(c + 1) * 128], ident[0:Q, 0:Q])
                    mm.then_inc(ring_full, 1)

            xnT_b = xnT[:, :, :].rearrange("p c (b h) -> p c b h", b=2)

            def queries(p):
                bank = ring_bank(p, "q", 0)
                for yc in range(C):
                    for xc in range(C):
                        pe.matmul(bank[:, yc * 2 * T:(yc + 1) * 2 * T], wqk[:, xc, yc * 128:(yc + 1) * 128],
                                  xnT_b[:, xc, :, 0:T], start=(xc == 0), stop=(xc == C - 1))
                for xc in range(C):
                    mm = pe.matmul(bank[0:R, C * 2 * T:C * 2 * T + 1], xnT[:, xc, 0:R], cvec[:, xc:xc + 1],
                                   start=(xc == 0), stop=(xc == C - 1))
                mm.then_inc(ring_full, 1)

            def transpose_probs(p):
                for g in range(GROUPS):
                    pe.wait_ge(exp_ready, p * GROUPS + g + 1)
                    bank = ring_bank(p + 1, "pT", g)
                    for k in range(KPG):
                        mm = pe.transpose(bank[0:Q, k * R:(k + 1) * R], probs[0:R, KPG * g + k, :], ident[0:R, 0:R])
                    mm.then_inc(ring_full, 1)

            def attend(p, par):
                if not (isinstance(p, int) and p == 0):
                    pe.wait_ge(x1_ready, p)
                for k in range(KT_N):
                    if k % KPG == 0:
                        evacuated(p + 1, "pT", k // KPG)
                    for b in range(2):
                        mm = pe.matmul(attended[b * HALF:b * HALF + T, :], probsT[0:Q, k, b * HALF:b * HALF + T],
                                       keys[par][0:Q, b, k, :], start=(k == 0), stop=(k == KT_N - 1))
                    if k % KPG == KPG - 1:
                        if k < KT_N - 1:
                            mm.then_inc(keys_used, 1)
                        else:
                            mm.then_inc(attended_ready, 1)

            def score(p, par, g):
                if g == 0 and not (isinstance(p, int) and p == 0):
                    pe.wait_ge(exp_ready, p * GROUPS)
                if g == 0:
                    evacuated(p, "q", 0)
                    evacuated(p, "kT0", 7)
                for c in range(C):
                    for b in range(2):
                        if g > 0:
                            evacuated(p, "kT%d" % g, 2 * c + b)
                    for b in range(2):
                        mm = pe.matmul(scores[b * HALF:b * HALF + T, g, 0:GK], qT[:, c, b, :],
                                       keysT[(par + g) % 2][:, b, c, :], start=(c == 0), stop=(c == C - 1))
                mm.then_inc(scores_ready, 1)

            def feed_forward(p):
                evacuated(p + 1, "yT", 0)
                if not (isinstance(p, int) and p == 0):
                    pe.wait_ge(result_ready, p)
                else:
                    pe.wait_ge(sign_loaded, 16)
                for c in range(C):
                    mm = pe.matmul(ffn[0:R, :], x1nT[:, c, :], signs[:, c, :], start=(c == 0), stop=(c == C - 1))
                mm.then_inc(ffn_ready, 1)

            pe.wait_ge(w_loaded, 32)
            pe.wait_ge(b_loaded, 32)
            for yc in range(C):
                for dc in range(C):
                    pe.matmul(ffn[:, yc:yc + 1], wk[:, dc, yc * 128:(yc + 1) * 128], bqc[:, dc:dc + 1],
                              start=(dc == 0), stop=(dc == C - 1))
            for xc in range(C):
                for dc in range(C):
                    pe.matmul(ffn[:, C + xc:C + xc + 1], wq[:, dc, xc * 128:(xc + 1) * 128], bkc[:, dc:dc + 1],
                              start=(dc == 0), stop=(dc == C - 1))
            pe.wait_ge(consts_ready, 4)
            pe.wait_ge(bsum_ready, 1)
            pe.matmul(ffn[:, 2 * C:2 * C + 1], ones[:, :], bsum[:, :], start=True, stop=True)
            pe.wait_ge(gain_loaded, 16)
            pe.matmul(ffn[:, 2 * C + 1:2 * C + 2], ones[0:1, :], gain_in[:, :], start=True,
                      stop=True).then_inc(setup_small, 1)
            for xc in range(C):
                for dc in range(C):
                    mm = pe.matmul(setup_bank(xc), wq[:, dc, xc * 128:(xc + 1) * 128], wk[:, dc, :],
                                   start=(dc == 0), stop=(dc == C - 1))
                mm.then_inc(setup_mm, 1)

            def step(p, par, half):
                first = isinstance(p, int) and p == 0
                transpose_x(p, xn, (xn_ready, p + 1), "xT")
                transpose_keys(p, par, half, 0)
                if first:
                    pe.wait_ge(setup_act, 2)
                    pe.wait_ge(setup_dve, 5)
                queries(p)
                if not first:
                    transpose_probs(p - 1)
                    attend(p - 1, 1 - par)
                transpose_keys(p, par, half, 1)
                if first:
                    pe.wait_ge(psum_zeroed, 2)
                score(p, par, 0)
                transpose_keys(p, par, half, 2)
                if not first:
                    transpose_x(p, x1n, (x1n_ready, p), "yT")
                score(p, par, 1)
                if not first:
                    feed_forward(p - 1)
                score(p, par, 2)

            over_steps(pe, step)
            transpose_probs(STEPS - 1)
            attend(STEPS - 1, 1)
            transpose_x(STEPS, x1n, (x1n_ready, STEPS), "yT")
            feed_forward(STEPS - 1)


_INS = ["x", "ctx_4096", "L0_xattn_Wq", "L0_xattn_bq", "L0_xattn_Wk", "L0_xattn_bk", "L0_ffn_sign", "L0_ffn_scale"]


def kernel(**inputs):
    import numpy as _np
    import concourse.bacc as _bacc
    from concourse import mybir as _mybir
    from concourse.bass_utils import run_bass_kernel_spmd as _run

    nc = _bacc.Bacc("TRN2", target_bir_lowering=False, num_devices=1)
    arrays, args = {}, []
    for name in _INS:
        a = _np.ascontiguousarray(inputs[name])
        if a.ndim == 0:
            a = a.reshape(1)
        arrays[f"in_{name}"] = a
        args.append(nc.dram_tensor(f"in_{name}", a.shape, _mybir.dt.from_np(a.dtype), kind="ExternalInput").ap())
    args.append(nc.dram_tensor("out_0", inputs["x"].shape, _mybir.dt.from_np(_np.dtype("float32")),
                               kind="ExternalOutput").ap())
    xattn_ffn_kernel(nc, *args)
    r = _run(nc, [arrays], core_ids=[0])
    return r.results[0]["out_0"]
```

```python
from contextlib import ExitStack

import concourse.bass as bass
from concourse import mybir

F32 = mybir.dt.float32
ALU = mybir.AluOpType
ACT = mybir.ActivationFunctionType
AX_X = mybir.AxisListType.X

HALF = 64
GROUPS = 3
PE_GROUPS = GROUPS - 1
RING = 4

SHARE = [("dve", "act")[i % 2] for i in range(8)]
KT_USES = [[("kT%d" % g, i, SHARE[i]) for i in range(8)] for g in range(PE_GROUPS)]
PT_USES = [("pT", 0, "act"), ("pT", 1, "dve"), ("pT", 2, "act")]
FFN_USES = [("yT", 0, "act"), ("ffn", 0, "dve")]
FIRST = [("xT", 0, "act")] + KT_USES[0] + [("q", 0, "dve")] + KT_USES[1]
STEADY = [("xT", 0, "act")] + KT_USES[0] + [("q", 0, "dve")] + PT_USES + KT_USES[1] + FFN_USES
TAIL = PT_USES + FFN_USES


def uses_of(steps, p):
    if isinstance(p, int) and p == 0:
        return FIRST
    return TAIL if isinstance(p, int) and p == steps else STEADY


def before_step(p, counted):
    if isinstance(p, int) and p == 0:
        return 0
    return (p - 1) * sum(map(counted, STEADY)) + sum(map(counted, FIRST))


def ring_position(steps, p, what, index):
    uses = uses_of(steps, p)
    at = [u[:2] for u in uses].index((what, index))
    engine = uses[at][2]
    return (at % RING, before_step(p, lambda u: True) + at + 1,
            before_step(p, lambda u: u[2] == engine) + sum(u[2] == engine for u in uses[:at + 1]), engine)


def ring_previous(steps, p, what, index):
    uses = uses_of(steps, p)
    at = [u[:2] for u in uses].index((what, index))
    if at >= RING:
        _, _, n, engine = ring_position(steps, p, *uses[at - RING][:2])
        return engine, n
    if uses is not FIRST and at == (len(STEADY) - 1) % RING:
        return "dve", before_step(p, lambda u: u[2] == "dve")
    return None


def xattn_ffn_kernel(nc, x, ctx_in, Wq, bq, Wk, bk, sign, scale, out):
    B, T, D = x.shape
    S = ctx_in.shape[1]
    STEPS = B // 2
    C = D // 128
    KT_N = 12
    Q = S // KT_N
    KPG = KT_N // GROUPS
    PAD = 128 - Q
    GK = KPG * Q
    SIDE = GROUPS - 1
    R = HALF + T
    SCALE = float(D) ** -0.5
    EPS = 1e-5
    MAIN = Q // 16 * 16
    assert Q * KT_N == S and Q <= 128 and GK <= 512 and T <= HALF and STEPS % 2 == 0

    x_v = x.rearrange("(n b) t d -> n b t d", b=2)
    out_v = out.rearrange("(n b) t d -> n b t d", b=2)
    ctx_v = ctx_in.rearrange("(n b) (g q k) d -> n g q b (k d)", b=2, g=GROUPS, k=KPG)
    side_v = ctx_in.rearrange("(n b) s d -> n b s d", b=2)[:, :, SIDE * GK - KPG * PAD:, :]
    side_v = side_v.rearrange("n b (r e) d -> n b r e d", r=32)

    with ExitStack() as stack:
        def sb(name, shape):
            return stack.enter_context(nc.sbuf_tensor(name, shape, F32))

        def pb(name, shape):
            return stack.enter_context(nc.psum_tensor(name, shape, F32))

        def sem(name):
            return stack.enter_context(nc.semaphore(name))

        keys = [sb(f"keys{i}", [128, 2, KT_N, D]) for i in range(2)]
        keysT = [sb(f"keysT{i}", [128, 2, C, GK]) for i in range(PE_GROUPS)]
        side = sb("side", [128, 2, 4, KPG, 128])
        sideT = sb("sideT", [128, 2, C, KPG, 128])
        wq = keys[1][:, 0, 0:C, :]
        wk = keys[1][:, 1, 0:C, :]
        bqc = sb("bqc", [128, C])
        bkc = sb("bkc", [128, C])
        bkrep = sideT[:, 0, 0, :, :]
        bprod = sb("bprod", [128, C])
        bsum = sb("bsum", [128, 1])
        wqk = sb("wqk", [128, C, D])
        qbias = sb("qbias", [128, C])
        crep = sb("crep", [128, D])
        cprod = stack.enter_context(nc.sbuf_tensor("cprod", [128, D], mybir.dt.bfloat16))
        cconst = sb("cconst", [128, 1])
        signs = sb("signs", [128, C, D])
        gain_in = sb("gain_in", [1, 1])
        gain = sb("gain", [128, 1])
        gabs = sb("gabs", [128, 1])
        gexp = sb("gexp", [128, 1])
        glog = sb("glog", [128, 1])
        softplus = sb("softplus", [128, 1])
        ones = sb("ones", [128, 128])
        ident = sb("ident", [128, 128])
        minus_half = sb("minus_half", [128, 1])
        eps = sb("eps", [128, 1])
        xs = [sb(f"xs{i}", [128, D]) for i in range(2)]
        xn = sb("xn", [128, D])
        xnT = sb("xnT", [128, C, 2 * HALF])
        qT = sb("qT", [128, C, 2, T])
        crow = sb("crow", [128, 1])
        gmax = sb("gmax", [128, GROUPS])
        smax = sb("smax", [128, 1])
        cmax = sb("cmax", [128, 1])
        ebias = sb("ebias", [128, 1])
        probs = sb("probs", [128, KT_N, Q])
        gsum = sb("gsum", [128, GROUPS])
        rsum = sb("rsum", [128, 1])
        rinv = sb("rinv", [128, 1])
        probsT = sb("probsT", [128, KT_N, R])
        x1 = sb("x1", [128, D])
        x1n = sb("x1n", [128, D])
        x1nT = sb("x1nT", [128, C, R])
        result = x1n
        xstat = sb("xstat", [128, 6])
        xmv = sb("xmv", [128, 2])
        xvar = sb("xvar", [128, 1])
        xrstd = sb("xrstd", [128, 1])
        ystat = sb("ystat", [128, 6])
        ymv = sb("ymv", [128, 2])
        yvar = sb("yvar", [128, 1])
        yrstd = sb("yrstd", [128, 1])

        scores = pb("scores", [128, GROUPS, 512])
        ring = [pb(f"ring{i}", [128, 512]) for i in range(RING)]
        attended = pb("attended", [128, 512])

        w_loaded = sem("w_loaded")
        b_loaded = sem("b_loaded")
        sign_loaded = sem("sign_loaded")
        gain_loaded = sem("gain_loaded")
        keys_loaded = [[sem(f"keys_loaded{i}_{g}") for g in range(GROUPS)] for i in range(2)]
        x_loaded = [sem(f"x_loaded{i}") for i in range(2)]
        out_stored = sem("out_stored")
        consts_ready = sem("consts_ready")
        ident_zero = sem("ident_zero")
        x_zeroed = sem("x_zeroed")
        bprod_ready = sem("bprod_ready")
        bsum_ready = sem("bsum_ready")
        setup_small = sem("setup_small")
        setup_mm = sem("setup_mm")
        setup_act = sem("setup_act")
        setup_dve = sem("setup_dve")
        psum_zeroed = sem("psum_zeroed")
        gain_copied = sem("gain_copied")
        gabs_ready = sem("gabs_ready")
        gexp_ready = sem("gexp_ready")
        glog_ready = sem("glog_ready")
        softplus_ready = sem("softplus_ready")
        smalls_copied = sem("smalls_copied")
        bkrep_ready = sem("bkrep_ready")
        side_loaded = sem("side_loaded")
        side_done = sem("side_done")
        ring_full = sem("ring_full")
        ring_act = sem("ring_act")
        ring_dve = sem("ring_dve")
        xstat_ready = sem("xstat_ready")
        xmv_ready = sem("xmv_ready")
        xvar_ready = sem("xvar_ready")
        xrstd_ready = sem("xrstd_ready")
        xn_ready = sem("xn_ready")
        ystat_ready = sem("ystat_ready")
        ymv_ready = sem("ymv_ready")
        yvar_ready = sem("yvar_ready")
        yrstd_ready = sem("yrstd_ready")
        x1_ready = sem("x1_ready")
        x1n_ready = sem("x1n_ready")
        crow_ready = sem("crow_ready")
        scores_ready = sem("scores_ready")
        gmax_ready = sem("gmax_ready")
        smax_ready = sem("smax_ready")
        cmax_ready = sem("cmax_ready")
        ebias_ready = sem("ebias_ready")
        exp_ready = sem("exp_ready")
        rsum_ready = sem("rsum_ready")
        rinv_ready = sem("rinv_ready")
        keys_used = sem("keys_used")
        attended_ready = sem("attended_ready")

        ring_sem = {"act": ring_act, "dve": ring_dve}

        block = stack.enter_context(nc.Block())

        def over_steps(engine, step):
            step(0, 0, 0)
            with engine.Fori(0, STEPS // 2 - 1) as i:
                step(i * 2 + 1, 1, i)
                step(i * 2 + 2, 0, i + 1)
            step(STEPS - 1, 1, STEPS // 2 - 1)

        @block.sync
        def _(sp):
            def load_keys(p, par, g):
                dst = keys[par][:, :, KPG * g:KPG * (g + 1), :].rearrange("q b k d -> q b (k d)")
                src = ctx_v[bass.ds(p, 1), g].rearrange("n q b e -> (n q) b e")
                for a, z in ((0, MAIN), (MAIN, Q)):
                    sp.dma_start(dst[a:z], src[a:z]).then_inc(keys_loaded[par][g], 16)

            def store(p):
                dst = out_v[bass.ds(p, 1)].rearrange("n b t d -> (n b) t d")
                for b in range(2):
                    sp.dma_start(dst[b], result[b * HALF:b * HALF + T, :]).then_inc(out_stored, 16)

            def load_x(p, par):
                src = x_v[bass.ds(p, 1)].rearrange("n b t d -> (n b) t d")
                for b in range(2):
                    sp.dma_start(xs[par][b * HALF:b * HALF + T, :], src[b]).then_inc(x_loaded[par], 16)

            def load_side(p):
                src = side_v[bass.ds(p, 1)].rearrange("n b r e d -> (n b) r e d")
                for b in range(2):
                    for i in range(4):
                        sp.dma_start(side[32 * i:32 * i + 32, b, :, :, :].rearrange("r s k d -> r (s k) d"),
                                     src[b, :, :, 128 * i:128 * i + 128]).then_inc(side_loaded, 16)

            sp.dma_start(bqc[:], bq.rearrange("(p c) -> p c", c=C)).then_inc(b_loaded, 16)
            sp.dma_start(bkc[:], bk.rearrange("(p c) -> p c", c=C)).then_inc(b_loaded, 16)
            sp.dma_start(gain_in[:], scale.rearrange("(a b) -> a b", a=1)).then_inc(gain_loaded, 16)
            sp.dma_start(wq, Wq.rearrange("(p c) x -> p c x", c=C)).then_inc(w_loaded, 16)
            sp.dma_start(wk, Wk.rearrange("(p c) x -> p c x", c=C)).then_inc(w_loaded, 16)
            sp.wait_ge(x_zeroed, 2)
            load_x(0, 0)
            load_keys(0, 0, 0)
            load_keys(0, 0, 1)
            load_side(0)
            load_keys(0, 0, 2)
            load_x(1, 1)
            sp.dma_start(signs[:], sign.rearrange("(c p) o -> p c o", p=128)).then_inc(sign_loaded, 16)
            sp.wait_ge(setup_mm, C)
            for g in range(GROUPS):
                load_keys(1, 1, g)
            sp.wait_ge(side_done, 2)
            load_side(1)

            def step(p, par):
                for g in range(GROUPS - 1):
                    sp.wait_ge(keys_used, (p - 1) * (GROUPS - 1) + g + 1)
                    load_keys(p + 1, 1 - par, g)
                sp.wait_ge(x1_ready, p)
                load_x(p + 1, 1 - par)
                load_keys(p + 1, 1 - par, SIDE)
                sp.wait_ge(side_done, 2 * (p + 1))
                load_side(p + 1)
                sp.wait_ge(ring_dve, ring_position(STEPS, p, "ffn", 0)[2])
                store(p - 1)

            with sp.Fori(0, STEPS // 2 - 1) as i:
                step(i * 2 + 1, 1)
                step(i * 2 + 2, 0)
            for p in (STEPS - 1, STEPS):
                sp.wait_ge(ring_dve, ring_position(STEPS, p, "ffn", 0)[2])
                store(p - 1)
            sp.wait_ge(out_stored, 32 * (STEPS + 1))

        @block.gpsimd
        def _(pool):
            nc.gpsimd.memset(xs[0][:], 0.0).then_inc(x_zeroed, 1)
            nc.gpsimd.memset(xs[1][:], 0.0).then_inc(x_zeroed, 1)
            nc.gpsimd.memset(ident[:], 0.0).then_inc(ident_zero, 1)
            nc.gpsimd.memset(ones[:], 1.0).then_inc(consts_ready, 1)
            nc.gpsimd.memset(minus_half[:], -0.5).then_inc(consts_ready, 1)
            nc.gpsimd.memset(eps[:], EPS).then_inc(consts_ready, 1)
            pool.wait_ge(ident_zero, 1)
            nc.gpsimd.affine_select(out=ident[:], in_=ident[:], compare_op=ALU.not_equal, fill=1.0, base=0,
                                    pattern=[[-1, 128]], channel_multiplier=1).then_inc(consts_ready, 1)
            pool.wait_ge(consts_ready, 3)

            def x_rstd(p):
                pool.wait_ge(xmv_ready, p + 1)
                nc.gpsimd.tensor_tensor(xvar[0:R, :], xmv[0:R, 1:2], eps[0:R, :], ALU.add).then_inc(xvar_ready, 1)
                pool.wait_ge(xvar_ready, p + 1)
                nc.gpsimd.tensor_tensor(xrstd[0:R, :], xvar[0:R, :], minus_half[0:R, :],
                                        ALU.pow).then_inc(xrstd_ready, 1)

            def y_rstd(p):
                pool.wait_ge(ymv_ready, p + 1)
                nc.gpsimd.tensor_tensor(yvar[0:R, :], ymv[0:R, 1:2], eps[0:R, :], ALU.add).then_inc(yvar_ready, 1)
                pool.wait_ge(yvar_ready, p + 1)
                nc.gpsimd.tensor_tensor(yrstd[0:R, :], yvar[0:R, :], minus_half[0:R, :],
                                        ALU.pow).then_inc(yrstd_ready, 1)

            x_rstd(0)
            x_rstd(1)
            def step(p, par):
                y_rstd(p - 1)
                x_rstd(p + 1)

            with pool.Fori(0, STEPS // 2 - 1) as i:
                step(i * 2 + 1, 1)
                step(i * 2 + 2, 0)
            y_rstd(STEPS - 2)
            y_rstd(STEPS - 1)

        def setup_bank(xc):
            return scores[:, xc, :] if xc < GROUPS else attended[:, :]

        def permuted(ap):
            return ap.rearrange("p (r c) -> p c r", c=C)

        def score_order(p):
            return (0, SIDE, 1) if isinstance(p, int) and p == 0 else (SIDE, 0, 1)

        def ring_take(engine, p, what, index):
            bank, n, _, _ = ring_position(STEPS, p, what, index)
            engine.wait_ge(ring_full, n)
            return ring[bank]

        @block.scalar
        def _(act):
            def copy(out_ap, in_ap):
                return nc.scalar.activation(out_ap, in_ap, ACT.Copy)

            def keys_evac(p, g, i):
                if SHARE[i] == "act":
                    bank = ring_take(act, p, "kT%d" % g, i)
                    copy(keysT[g][:, i % 2, i // 2, :], bank[:, 0:GK]).then_inc(ring_act, 1)

            def x_evac(p):
                bank = ring_take(act, p, "xT", 0)
                copy(xnT[:, :, 0:R], bank[:, 0:C * R].rearrange("p (c r) -> p c r", c=C)).then_inc(ring_act, 1)

            def exps(p, g):
                if g == 0:
                    act.wait_ge(ebias_ready, p + 1)
                nc.scalar.activation(probs[0:R, KPG * g:KPG * (g + 1), :],
                                     scores[0:R, g, 0:GK].rearrange("r (k q) -> r k q", q=Q), ACT.Exp,
                                     bias=ebias[0:R, :], scale=1.0,
                                     accum_out=gsum[0:R, g:g + 1]).then_inc(exp_ready, 1)

            def probs_evac(p, g):
                bank = ring_take(act, p + 1, "pT", g)
                copy(probsT[0:Q, KPG * g:KPG * (g + 1), :],
                     bank[0:Q, 0:KPG * R].rearrange("q (k r) -> q k r", r=R)).then_inc(ring_act, 1)

            act.wait_ge(gabs_ready, 1)
            nc.scalar.activation(gexp[:], gabs[:], ACT.Exp, scale=-1.0).then_inc(gexp_ready, 1)
            act.wait_ge(gexp_ready, 1)
            nc.scalar.activation(glog[:], gexp[:], ACT.Ln, bias=1.0).then_inc(glog_ready, 1)
            for xc in (0, 2):
                act.wait_ge(setup_mm, xc + 1)
                nc.scalar.activation(wqk[:, xc, :].rearrange("p (c r) -> p c r", c=C),
                                     permuted(setup_bank(xc)), ACT.Copy, scale=SCALE).then_inc(setup_act, 1)

            def y_evac(p):
                bank = ring_take(act, p + 1, "yT", 0)
                copy(x1nT[:, :, :], bank[:, 0:C * R].rearrange("p (c r) -> p c r", c=C)).then_inc(ring_act, 1)

            def step(p, par, half):
                first = isinstance(p, int) and p == 0
                x_evac(p)
                for i in range(8):
                    keys_evac(p, 0, i)
                if not first:
                    probs_evac(p - 1, 0)
                    probs_evac(p - 1, 2)
                for i in range(8):
                    keys_evac(p, 1, i)
                if not first:
                    y_evac(p - 1)
                for g in range(GROUPS):
                    exps(p, g)

            over_steps(act, step)
            probs_evac(STEPS - 1, 0)
            probs_evac(STEPS - 1, 2)
            y_evac(STEPS - 1)

        @block.vector
        def _(dve):
            def keys_evac(p, g, i):
                if SHARE[i] == "dve":
                    bank = ring_take(dve, p, "kT%d" % g, i)
                    nc.vector.tensor_copy(keysT[g][:, i % 2, i // 2, :],
                                          bank[:, 0:GK]).then_inc(ring_dve, 1)

            def group_max(p, g):
                dve.wait_ge(scores_ready, p * GROUPS + score_order(p).index(g) + 1)
                nc.vector.reduce_max(gmax[0:R, g:g + 1], scores[0:R, g, 0:GK], AX_X).then_inc(gmax_ready, 1)

            def softmax_bias(p):
                dve.wait_ge(gmax_ready, (p + 1) * GROUPS)
                nc.vector.reduce_max(smax[0:R, :], gmax[0:R, :], AX_X).then_inc(smax_ready, 1)
                dve.wait_ge(smax_ready, p + 1)
                dve.wait_ge(crow_ready, p + 1)
                nc.vector.tensor_tensor(cmax[0:R, :], smax[0:R, :], crow[0:R, :], ALU.add).then_inc(cmax_ready, 1)
                dve.wait_ge(cmax_ready, p + 1)
                nc.vector.tensor_tensor(ebias[0:R, :], crow[0:R, :], cmax[0:R, :],
                                        ALU.subtract).then_inc(ebias_ready, 1)

            def x_stats(p, par, half):
                dve.wait_ge(x_loaded[par], half * 32 + 32)
                nc.vector.bn_stats(xstat[0:R, :], xs[par][0:R, :]).then_inc(xstat_ready, 1)

            def x_aggregate(p):
                nc.vector.bn_aggr(xmv[0:R, :], xstat[0:R, :]).then_inc(xmv_ready, 1)

            def x_normalise(p, par):
                dve.wait_ge(xrstd_ready, p + 1)
                if not (isinstance(p, int) and p == 0):
                    dve.wait_ge(ring_full, ring_position(STEPS, p - 1, "xT", 0)[1])
                nc.vector.tensor_scalar(xn[0:R, :], xs[par][0:R, :], xmv[0:R, 0:1], xrstd[0:R, :],
                                        ALU.subtract, ALU.mult).then_inc(xn_ready, 1)

            def q_evac(p):
                bank = ring_take(dve, p, "q", 0)
                nc.vector.tensor_tensor(qT[:, :, :, :].rearrange("p c b t -> p c (b t)"),
                                        bank[:, 0:C * 2 * T].rearrange("p (c n) -> p c n", c=C),
                                        qbias[:, :].rearrange("p (c o) -> p c o", o=1).to_broadcast([128, C, 2 * T]),
                                        ALU.add).then_inc(ring_dve, 1)

            def c_column(p):
                nc.vector.tensor_tensor_reduce(out=cprod[0:R, :], in0=xn[0:R, :], in1=crep[0:R, :], scale=1.0,
                                               scalar=cconst[0:R, :], op0=ALU.mult, op1=ALU.add,
                                               accum_out=crow[0:R, :]).then_inc(crow_ready, 1)

            def side_transposes(p):
                dve.wait_ge(side_loaded, p * 128 + 128)
                for b in range(2):
                    for k in range(KPG):
                        tr = nc.vector.transpose(sideT[:, b, :, k, :].rearrange("p c (r s) -> p s c r", s=4),
                                                 side[:, b, :, k, :].rearrange("p s (a c) -> p s c a", c=C))
                    tr.then_inc(side_done, 1)

            def row_sums(p):
                dve.wait_ge(exp_ready, (p + 1) * GROUPS)
                nc.vector.reduce_sum(rsum[0:R, :], gsum[0:R, :], AX_X).then_inc(rsum_ready, 1)
                dve.wait_ge(rsum_ready, p + 1)
                nc.vector.reciprocal(rinv[0:R, :], rsum[0:R, :]).then_inc(rinv_ready, 1)

            def probs_evac(p, g):
                bank = ring_take(dve, p + 1, "pT", g)
                nc.vector.tensor_copy(probsT[0:Q, KPG * g:KPG * (g + 1), :],
                                      bank[0:Q, 0:KPG * R].rearrange("q (k r) -> q k r", r=R)).then_inc(ring_dve, 1)

            def residual(p, par):
                dve.wait_ge(attended_ready, p + 1)
                dve.wait_ge(rinv_ready, p + 1)
                nc.vector.scalar_tensor_tensor(out=x1[0:R, :], in0=attended[0:R, :], scalar=rinv[0:R, :],
                                               in1=xs[par][0:R, :], op0=ALU.mult, op1=ALU.add).then_inc(x1_ready, 1)

            def x1_stats(p):
                dve.wait_ge(x1_ready, p + 1)
                nc.vector.bn_stats(ystat[0:R, :], x1[0:R, :]).then_inc(ystat_ready, 1)

            def x1_aggregate(p):
                nc.vector.bn_aggr(ymv[0:R, :], ystat[0:R, :]).then_inc(ymv_ready, 1)

            def x1_normalise(p):
                dve.wait_ge(out_stored, p * 32 + 32)
                dve.wait_ge(yrstd_ready, p + 1)
                nc.vector.tensor_scalar(x1n[0:R, :], x1[0:R, :], ymv[0:R, 0:1], yrstd[0:R, :],
                                        ALU.subtract, ALU.mult).then_inc(x1n_ready, 1)

            def finish(p):
                bank = ring_take(dve, p + 1, "ffn", 0)
                nc.vector.scalar_tensor_tensor(out=result[0:R, :], in0=bank[0:R, :], scalar=softplus[0:R, :],
                                               in1=x1[0:R, :], op0=ALU.mult, op1=ALU.add).then_inc(ring_dve, 1)

            dve.wait_ge(b_loaded, 32)
            nc.vector.tensor_tensor(bprod[:], bqc[:], bkc[:], ALU.mult).then_inc(bprod_ready, 1)
            dve.wait_ge(consts_ready, 4)
            for dc in range(C):
                nc.vector.tensor_scalar(bkrep[:, dc, :], ones[:], bkc[:, dc:dc + 1], None,
                                        ALU.mult).then_inc(bkrep_ready, 1)
            dve.wait_ge(bprod_ready, 1)
            nc.vector.reduce_sum(bsum[:], bprod[:], AX_X).then_inc(bsum_ready, 1)
            dve.wait_ge(setup_small, 1)
            nc.vector.tensor_scalar(qbias[:], ring[0][:, 0:C], SCALE, None, ALU.mult).then_inc(smalls_copied, 1)
            nc.vector.tensor_scalar(cconst[:], ring[0][:, C:C + 1], SCALE, None, ALU.mult).then_inc(smalls_copied, 1)
            nc.vector.tensor_scalar(crep[:], ring[1][:, :], SCALE, None, ALU.mult).then_inc(smalls_copied, 1)
            nc.vector.tensor_copy(gain[:], ring[0][:, C + 1:C + 2]).then_inc(gain_copied, 1)
            dve.wait_ge(gain_copied, 1)
            nc.vector.scalar_tensor_tensor(out=gabs[:], in0=gain[:], scalar=-1.0, in1=gain[:],
                                           op0=ALU.mult, op1=ALU.max).then_inc(gabs_ready, 1)
            x_stats(0, 0, 0)
            dve.wait_ge(xstat_ready, 1)
            x_aggregate(0)
            x_normalise(0, 0)
            for xc in (1, 3):
                dve.wait_ge(setup_mm, xc + 1)
                nc.vector.tensor_scalar(wqk[:, xc, :].rearrange("p (c r) -> p c r", c=C),
                                        permuted(setup_bank(xc)), SCALE, None, ALU.mult).then_inc(setup_dve, 1)
            dve.wait_ge(glog_ready, 1)
            nc.vector.scalar_tensor_tensor(out=softplus[:], in0=gain[:], scalar=0.0, in1=glog[:],
                                           op0=ALU.max, op1=ALU.add).then_inc(softplus_ready, 1)
            dve.wait_ge(setup_dve, 2)
            dve.wait_ge(setup_act, 2)
            nc.vector.memset(scores[:, :, :], 0.0).then_inc(psum_zeroed, 1)
            nc.vector.memset(attended[:, :], 0.0).then_inc(psum_zeroed, 1)
            nc.vector.memset(result[:], 0.0).then_inc(out_stored, 32)
            dve.wait_ge(softplus_ready, 1)
            dve.wait_ge(psum_zeroed, 2)
            dve.wait_ge(smalls_copied, 3)

            def step(p, par, half, last=False):
                first = isinstance(p, int) and p == 0
                for i in range(8):
                    keys_evac(p, 0, i)
                q_evac(p)
                if first:
                    c_column(p)
                    for i in range(8):
                        keys_evac(p, 1, i)
                    side_transposes(p)
                else:
                    row_sums(p - 1)
                    probs_evac(p - 1, 1)
                    side_transposes(p)
                    residual(p - 1, 1 - par)
                    x1_stats(p - 1)
                    dve.wait_ge(ystat_ready, p)
                    c_column(p)
                    x1_aggregate(p - 1)
                    group_max(p, SIDE)
                    x1_normalise(p - 1)
                    for i in range(8):
                        keys_evac(p, 1, i)
                if not last:
                    x_stats(p + 1, 1 - par, half if par == 0 else half + 1)
                    dve.wait_ge(xstat_ready, p + 2)
                group_max(p, 0)
                if first:
                    group_max(p, SIDE)
                if not last:
                    x_aggregate(p + 1)
                    x_normalise(p + 1, 1 - par)
                group_max(p, 1)
                softmax_bias(p)
                if not first:
                    finish(p - 1)

            step(0, 0, 0)
            with dve.Fori(0, STEPS // 2 - 1) as i:
                step(i * 2 + 1, 1, i)
                step(i * 2 + 2, 0, i + 1)
            step(STEPS - 1, 1, STEPS // 2 - 1, last=True)
            p = STEPS - 1
            row_sums(p)
            probs_evac(p, 1)
            residual(p, 1)
            x1_stats(p)
            dve.wait_ge(ystat_ready, p + 1)
            x1_aggregate(p)
            x1_normalise(p)
            finish(p)

        @block.tensor
        def _(pe):
            def ring_bank(p, what, index):
                previous = ring_previous(STEPS, p, what, index)
                if previous:
                    pe.wait_ge(ring_sem[previous[0]], previous[1])
                return ring[ring_position(STEPS, p, what, index)[0]]

            def evacuated(p, what, index):
                _, _, n, engine = ring_position(STEPS, p, what, index)
                pe.wait_ge(ring_sem[engine], n)

            def transpose_x(p, src, ready, what):
                pe.wait_ge(ready[0], ready[1])
                bank = ring_bank(p, what, 0)
                for c in range(C):
                    mm = pe.transpose(bank[:, c * R:(c + 1) * R], src[0:R, c * 128:(c + 1) * 128], ident[0:R, 0:R])
                mm.then_inc(ring_full, 1)

            def transpose_keys(p, par, half, g):
                pe.wait_ge(keys_loaded[par][g], half * 32 + 32)
                for i in range(8):
                    b, c = i % 2, i // 2
                    bank = ring_bank(p, "kT%d" % g, i)
                    for k in range(KPG):
                        mm = pe.transpose(bank[:, k * Q:(k + 1) * Q],
                                          permuted(keys[par][0:Q, b, KPG * g + k, :])[:, c], ident[0:Q, 0:Q])
                    mm.then_inc(ring_full, 1)

            xnT_b = xnT[:, :, :].rearrange("p c (b h) -> p c b h", b=2)

            def queries(p):
                bank = ring_bank(p, "q", 0)
                for yc in range(C):
                    for xc in range(C):
                        mm = pe.matmul(bank[:, yc * 2 * T:(yc + 1) * 2 * T], wqk[:, xc, yc * 128:(yc + 1) * 128],
                                       xnT_b[:, xc, :, 0:T], start=(xc == 0), stop=(xc == C - 1))
                mm.then_inc(ring_full, 1)

            def transpose_probs(p):
                for g in range(GROUPS):
                    pe.wait_ge(exp_ready, p * GROUPS + g + 1)
                    bank = ring_bank(p + 1, "pT", g)
                    for k in range(KPG):
                        mm = pe.transpose(bank[0:Q, k * R:(k + 1) * R], probs[0:R, KPG * g + k, :], ident[0:R, 0:R])
                    mm.then_inc(ring_full, 1)

            def attend(p, par, half):
                pe.wait_ge(keys_loaded[par][SIDE], half * 32 + 32)
                for k in range(KT_N):
                    if k % KPG == 0:
                        evacuated(p + 1, "pT", k // KPG)
                    for b in range(2):
                        mm = pe.matmul(attended[b * HALF:b * HALF + T, :], probsT[0:Q, k, b * HALF:b * HALF + T],
                                       keys[par][0:Q, b, k, :], start=(k == 0), stop=(k == KT_N - 1))
                    if k % KPG == KPG - 1:
                        if k < KT_N - 1:
                            mm.then_inc(keys_used, 1)
                        else:
                            mm.then_inc(attended_ready, 1)

            def score(p, g):
                if g == score_order(p)[0] and not (isinstance(p, int) and p == 0):
                    pe.wait_ge(exp_ready, p * GROUPS)
                if g == SIDE:
                    pe.wait_ge(side_done, 2 * (p + 1))
                if g == 0:
                    evacuated(p, "kT0", 7)
                if g == score_order(p)[0]:
                    evacuated(p, "q", 0)
                for c in range(C):
                    for b in range(2):
                        if g == 1:
                            evacuated(p, "kT1", 2 * c + b)
                    for b in range(2):
                        columns = sideT[:, b, c, :, PAD:] if g == SIDE else keysT[g][:, b, c, :]
                        mm = pe.matmul(scores[b * HALF:b * HALF + T, g, 0:GK], qT[:, c, b, :], columns,
                                       start=(c == 0), stop=(c == C - 1))
                mm.then_inc(scores_ready, 1)

            def feed_forward(p):
                if isinstance(p, int) and p == 0:
                    pe.wait_ge(sign_loaded, 16)
                evacuated(p + 1, "yT", 0)
                bank = ring_bank(p + 1, "ffn", 0)
                for c in range(C):
                    mm = pe.matmul(bank[0:R, :], x1nT[:, c, :], signs[:, c, :], start=(c == 0), stop=(c == C - 1))
                mm.then_inc(ring_full, 1)

            pe.wait_ge(w_loaded, 32)
            pe.wait_ge(b_loaded, 32)
            for yc in range(C):
                for dc in range(C):
                    pe.matmul(ring[0][:, yc:yc + 1], permuted(wk[:, dc, :])[:, yc], bqc[:, dc:dc + 1],
                              start=(dc == 0), stop=(dc == C - 1))
            pe.wait_ge(bkrep_ready, C)
            for dc in range(C):
                pe.matmul(ring[1][:, :], bkrep[:, dc, :], wq[:, dc, :], start=(dc == 0), stop=(dc == C - 1))
            pe.wait_ge(consts_ready, 4)
            pe.wait_ge(bsum_ready, 1)
            pe.matmul(ring[0][:, C:C + 1], ones[:, :], bsum[:, :], start=True, stop=True)
            pe.wait_ge(gain_loaded, 16)
            pe.matmul(ring[0][:, C + 1:C + 2], ones[0:1, :], gain_in[:, :], start=True,
                      stop=True).then_inc(setup_small, 1)
            for xc in range(C):
                for dc in range(C):
                    mm = pe.matmul(setup_bank(xc), wq[:, dc, xc * 128:(xc + 1) * 128], wk[:, dc, :],
                                   start=(dc == 0), stop=(dc == C - 1))
                mm.then_inc(setup_mm, 1)

            def step(p, par, half):
                first = isinstance(p, int) and p == 0
                if first:
                    pe.wait_ge(smalls_copied, 3)
                    pe.wait_ge(gain_copied, 1)
                transpose_x(p, xn, (xn_ready, p + 1), "xT")
                transpose_keys(p, par, half, 0)
                if first:
                    pe.wait_ge(setup_act, 2)
                    pe.wait_ge(setup_dve, 2)
                queries(p)
                if first:
                    transpose_keys(p, par, half, 1)
                    pe.wait_ge(psum_zeroed, 2)
                    for g in score_order(p):
                        score(p, g)
                else:
                    transpose_probs(p - 1)
                    attend(p - 1, 1 - par, half if par == 1 else half - 1)
                    score(p, SIDE)
                    transpose_keys(p, par, half, 1)
                    score(p, 0)
                    transpose_x(p, x1n, (x1n_ready, p), "yT")
                    score(p, 1)
                    feed_forward(p - 1)

            over_steps(pe, step)
            transpose_probs(STEPS - 1)
            attend(STEPS - 1, 1, STEPS // 2 - 1)
            transpose_x(STEPS, x1n, (x1n_ready, STEPS), "yT")
            feed_forward(STEPS - 1)


_INS = ["x", "ctx_4096", "L0_xattn_Wq", "L0_xattn_bq", "L0_xattn_Wk", "L0_xattn_bk", "L0_ffn_sign", "L0_ffn_scale"]


def kernel(**inputs):
    import numpy as _np
    import concourse.bacc as _bacc
    from concourse import mybir as _mybir
    from concourse.bass_utils import run_bass_kernel_spmd as _run

    nc = _bacc.Bacc("TRN2", target_bir_lowering=False, num_devices=1)
    arrays, args = {}, []
    for name in _INS:
        a = _np.ascontiguousarray(inputs[name])
        if a.ndim == 0:
            a = a.reshape(1)
        arrays[f"in_{name}"] = a
        args.append(nc.dram_tensor(f"in_{name}", a.shape, _mybir.dt.from_np(a.dtype), kind="ExternalInput").ap())
    args.append(nc.dram_tensor("out_0", inputs["x"].shape, _mybir.dt.from_np(_np.dtype("float32")),
                               kind="ExternalOutput").ap())
    xattn_ffn_kernel(nc, *args)
    r = _run(nc, [arrays], core_ids=[0])
    return r.results[0]["out_0"]
```

```python
from contextlib import ExitStack

import concourse.bass as bass
from concourse import mybir

F32 = mybir.dt.float32
F32R = mybir.dt.float32r
ALU = mybir.AluOpType
ACT = mybir.ActivationFunctionType
AX_X = mybir.AxisListType.X

HALF = 64
GROUPS = 3
RING = 4

KT_USES = [("kT", i, ("dve", "act")[i % 2]) for i in range(8)]
PT_USES = [("pT", 0, "act"), ("pT", 1, "dve"), ("pT", 2, "act")]
FFN_USES = [("yT", 0, "dve"), ("ffn", 0, "dve")]
FIRST = [("xT", 0, "act")] + [("kT", i, "act") for i in range(8)]
FIRST.insert(-2, ("q", 0, "dve"))
STEADY = [("xT", 0, "act")] + KT_USES + [("q", 0, "dve")] + PT_USES + FFN_USES
TAIL = PT_USES + FFN_USES


def uses_of(steps, p):
    if isinstance(p, int) and p == 0:
        return FIRST
    return TAIL if isinstance(p, int) and p == steps else STEADY


def before_step(p, counted):
    if isinstance(p, int) and p == 0:
        return 0
    return (p - 1) * sum(map(counted, STEADY)) + sum(map(counted, FIRST))


def ring_position(steps, p, what, index):
    uses = uses_of(steps, p)
    at = [u[:2] for u in uses].index((what, index))
    engine = uses[at][2]
    return (at % RING, before_step(p, lambda u: True) + at + 1,
            before_step(p, lambda u: u[2] == engine) + sum(u[2] == engine for u in uses[:at + 1]), engine)


def ring_previous(steps, p, what, index):
    uses = uses_of(steps, p)
    at = [u[:2] for u in uses].index((what, index))
    if at >= RING:
        _, _, n, engine = ring_position(steps, p, *uses[at - RING][:2])
        return engine, n
    if uses is not FIRST and at == (len(STEADY) - 1) % RING:
        return "dve", before_step(p, lambda u: u[2] == "dve")
    return None


def xattn_ffn_kernel(nc, x, ctx_in, Wq, bq, Wk, bk, sign, scale, out):
    B, T, D = x.shape
    S = ctx_in.shape[1]
    STEPS = B // 2
    C = D // 128
    KT_N = 12
    Q = S // KT_N
    KPG = KT_N // GROUPS
    PAD = 128 - Q
    GK = KPG * Q
    UNITS = 2 * (GROUPS - 1)
    ORDER = (1, 2, 0)
    R = HALF + T
    SCALE = float(D) ** -0.5
    EPS = 1e-5
    MAIN = Q // 16 * 16
    assert Q * KT_N == S and Q <= 128 and GK <= 512 and T <= HALF and STEPS % 2 == 0

    x_v = x.rearrange("(n b) t d -> n b t d", b=2)
    out_v = out.rearrange("(n b) t d -> n b t d", b=2)
    ctx_v = ctx_in.rearrange("(n b) (g q k) d -> n g q b (k d)", b=2, g=GROUPS, k=KPG)
    side_v = {g: ctx_in.rearrange("(n b) s d -> n b s d", b=2)[:, :, g * GK - KPG * PAD:(g + 1) * GK, :].rearrange(
        "n b (r e) d -> n b r e d", r=32) for g in range(1, GROUPS)}

    with ExitStack() as stack:
        def sb(name, shape):
            return stack.enter_context(nc.sbuf_tensor(name, shape, F32))

        def sb_r(name, shape):
            return stack.enter_context(nc.sbuf_tensor(name, shape, F32R))

        def pb(name, shape):
            return stack.enter_context(nc.psum_tensor(name, shape, F32))

        def sem(name):
            return stack.enter_context(nc.semaphore(name))

        keys = [sb(f"keys{i}", [128, 2, KT_N, D]) for i in range(2)]
        keysT = sb("keysT", [128, 2, C, GK])
        side = [sb(f"side{i}", [128, 4, KPG, 128]) for i in range(2)]
        sideT = [None] + [sb(f"sideT{g}", [128, 2, C, KPG, 128]) for g in range(1, GROUPS)]
        wq = keys[1][:, 0, 0:C, :]
        wk = keys[1][:, 1, 0:C, :]
        bqc = sb("bqc", [128, C])
        bkc = sb("bkc", [128, C])
        probs = sideT[2][:, 0, :, :, :].rearrange("p c k q -> p (c k q)")[:, 0:S].rearrange(
            "p (k q) -> p k q", q=Q)
        xn = sideT[2][:, 1, 0, :, :].rearrange("p k q -> p (k q)")
        xnT = sideT[2][:, 1, 1, :, :]
        cprod = sideT[2][:, 1, 2, :, :].rearrange("p k q -> p (k q)")
        bkrep = sideT[2][:, 1, 3, :, :]
        bprod = sb("bprod", [128, C])
        bsum = sb("bsum", [128, 1])
        wqk = sb("wqk", [128, C, D])
        qbias = sb("qbias", [128, C])
        crep = sb("crep", [128, D])
        cconst = sb("cconst", [128, 1])
        signs = keys[1][:, 0, KPG:KPG + C, :]
        signs_high = sb_r("signs_high", [128, C, D])
        signs_low = sb_r("signs_low", [128, C, D])
        gain_in = sb("gain_in", [1, 1])
        gain = sb("gain", [128, 1])
        gabs = sb("gabs", [128, 1])
        gexp = sb("gexp", [128, 1])
        glog = sb("glog", [128, 1])
        softplus = sb("softplus", [128, 1])
        ones = sb("ones", [128, 128])
        ident = sb("ident", [128, 128])
        minus_half = sb("minus_half", [128, 1])
        eps = sb("eps", [128, 1])
        xs = [sb(f"xs{i}", [128, D]) for i in range(2)]
        qT = sb("qT", [128, C, 2, T])
        crow = sb("crow", [128, 1])
        gmax = sb("gmax", [128, GROUPS])
        smax = sb("smax", [128, 1])
        cmax = sb("cmax", [128, 1])
        ebias = sb("ebias", [128, 1])
        gsum = sb("gsum", [128, GROUPS])
        rsum = sb("rsum", [128, 1])
        rinv = sb("rinv", [128, 1])
        probsT = sb("probsT", [128, KT_N, R])
        x1 = sb("x1", [128, D])
        x1n = sb("x1n", [128, D])
        x1nT_high = sb_r("x1nT_high", [128, C, R])
        x1nT_low = sb_r("x1nT_low", [128, C, R])
        result = x1n
        xstat = sb("xstat", [128, 6])
        xmv = sb("xmv", [128, 2])
        xvar = sb("xvar", [128, 1])
        xrstd = sb("xrstd", [128, 1])
        ystat = sb("ystat", [128, 6])
        ymv = sb("ymv", [128, 2])
        yvar = sb("yvar", [128, 1])
        yrstd = sb("yrstd", [128, 1])

        scores = pb("scores", [128, GROUPS, 512])
        ring = [pb(f"ring{i}", [128, 512]) for i in range(RING)]
        attended = pb("attended", [128, 512])

        wk_loaded = sem("wk_loaded")
        wq_loaded = sem("wq_loaded")
        b_loaded = sem("b_loaded")
        sign_loaded = sem("sign_loaded")
        signs_high_ready = sem("signs_high_ready")
        signs_split = sem("signs_split")
        y_high_ready = sem("y_high_ready")
        gain_loaded = sem("gain_loaded")
        keys_loaded = [[sem(f"keys_loaded{i}_{g}") for g in range(GROUPS)] for i in range(2)]
        x_loaded = [sem(f"x_loaded{i}") for i in range(2)]
        out_stored = sem("out_stored")
        consts_ready = sem("consts_ready")
        ident_zero = sem("ident_zero")
        x_zeroed = sem("x_zeroed")
        bprod_ready = sem("bprod_ready")
        bsum_ready = sem("bsum_ready")
        setup_small = sem("setup_small")
        setup_mm = sem("setup_mm")
        setup_act = sem("setup_act")
        setup_dve = sem("setup_dve")
        psum_zeroed = sem("psum_zeroed")
        gain_copied = sem("gain_copied")
        gabs_ready = sem("gabs_ready")
        gexp_ready = sem("gexp_ready")
        glog_ready = sem("glog_ready")
        softplus_ready = sem("softplus_ready")
        smalls_copied = sem("smalls_copied")
        bkrep_ready = sem("bkrep_ready")
        side_loaded = [sem(f"side_loaded{i}") for i in range(2)]
        side_done = sem("side_done")
        ring_full = sem("ring_full")
        ring_act = sem("ring_act")
        ring_dve = sem("ring_dve")
        xstat_ready = sem("xstat_ready")
        xmv_ready = sem("xmv_ready")
        xvar_ready = sem("xvar_ready")
        xrstd_ready = sem("xrstd_ready")
        xn_ready = sem("xn_ready")
        ystat_ready = sem("ystat_ready")
        ymv_ready = sem("ymv_ready")
        yvar_ready = sem("yvar_ready")
        yrstd_ready = sem("yrstd_ready")
        x1_ready = sem("x1_ready")
        x1n_ready = sem("x1n_ready")
        crow_ready = sem("crow_ready")
        scores_ready = sem("scores_ready")
        gmax_ready = sem("gmax_ready")
        smax_ready = sem("smax_ready")
        cmax_ready = sem("cmax_ready")
        ebias_ready = sem("ebias_ready")
        exp_ready = sem("exp_ready")
        rsum_ready = sem("rsum_ready")
        rinv_ready = sem("rinv_ready")
        attended_ready = sem("attended_ready")

        ring_sem = {"act": ring_act, "dve": ring_dve}

        block = stack.enter_context(nc.Block())

        def over_steps(engine, step):
            step(0, 0, 0)
            with engine.Fori(0, STEPS // 2 - 1) as i:
                step(i * 2 + 1, 1, i)
                step(i * 2 + 2, 0, i + 1)
            step(STEPS - 1, 1, STEPS // 2 - 1)

        @block.sync
        def _(sp):
            def load_keys(p, par, g, ahead=0):
                dst = keys[par][:, :, KPG * g:KPG * (g + 1), :].rearrange("q b k d -> q b (k d)")
                src = ctx_v[ahead:][bass.ds(p, 1), g].rearrange("n q b e -> (n q) b e")
                for a, z in ((0, MAIN), (MAIN, Q)):
                    sp.dma_start(dst[a:z], src[a:z]).then_inc(keys_loaded[par][g], 16)

            def store(p):
                dst = out_v[bass.ds(p, 1)].rearrange("n b t d -> (n b) t d")
                for b in range(2):
                    sp.dma_start(dst[b], result[b * HALF:b * HALF + T, :]).then_inc(out_stored, 16)

            def load_x(p, par):
                src = x_v[bass.ds(p, 1)].rearrange("n b t d -> (n b) t d")
                for b in range(2):
                    sp.dma_start(xs[par][b * HALF:b * HALF + T, :], src[b]).then_inc(x_loaded[par], 16)

            def load_side(p, unit, ahead=0):
                g, b = 1 + unit // 2, unit % 2
                src = side_v[g][ahead:][bass.ds(p, 1), b].rearrange("n r e d -> (n r) e d")
                for i in range(4):
                    sp.dma_start(side[unit % 2][32 * i:32 * i + 32, :, :, :].rearrange("r s k d -> r (s k) d"),
                                 src[:, :, 128 * i:128 * i + 128]).then_inc(side_loaded[unit % 2], 16)

            sp.dma_start(wk, Wk.rearrange("(p c) x -> p c x", c=C)).then_inc(wk_loaded, 16)
            sp.dma_start(bqc[:], bq.rearrange("(p c) -> p c", c=C)).then_inc(b_loaded, 16)
            sp.dma_start(bkc[:], bk.rearrange("(p c) -> p c", c=C)).then_inc(b_loaded, 16)
            sp.dma_start(wq, Wq.rearrange("(p c) x -> p c x", c=C)).then_inc(wq_loaded, 16)
            sp.dma_start(gain_in[:], scale.rearrange("(a b) -> a b", a=1)).then_inc(gain_loaded, 16)
            sp.wait_ge(x_zeroed, 2)
            load_x(0, 0)
            load_x(1, 1)
            load_side(0, 0)
            load_side(0, 1)
            load_keys(0, 0, 0)
            for unit in (2, 3):
                sp.wait_ge(side_done, unit - 1)
                load_side(0, unit)
            sp.dma_start(signs, sign.rearrange("(c p) o -> p c o", p=128)).then_inc(sign_loaded, 16)
            sp.wait_ge(setup_mm, C)
            load_keys(1, 1, 0)
            for unit in (0, 1):
                sp.wait_ge(side_done, unit + 3)
                load_side(1, unit)
            load_keys(0, 0, 1)
            load_keys(0, 0, 2)
            for unit in (2, 3):
                sp.wait_ge(side_done, UNITS + unit - 1)
                load_side(1, unit)
            sp.wait_ge(signs_split, 1)
            load_keys(1, 1, 1)

            def step(p, par):
                load_keys(p, par, 2)
                for unit in (0, 1):
                    sp.wait_ge(side_done, p * UNITS + unit + 3)
                    load_side(p, unit, ahead=1)
                sp.wait_ge(x1_ready, p)
                load_x(p + 1, 1 - par)
                load_keys(p, 1 - par, 0, ahead=1)
                for unit in (2, 3):
                    sp.wait_ge(side_done, p * UNITS + UNITS + unit - 1)
                    load_side(p, unit, ahead=1)
                load_keys(p, 1 - par, 1, ahead=1)
                sp.wait_ge(ring_dve, ring_position(STEPS, p, "ffn", 0)[2])
                store(p - 1)

            with sp.Fori(0, STEPS // 2 - 1) as i:
                step(i * 2 + 1, 1)
                step(i * 2 + 2, 0)
            load_keys(STEPS - 1, 1, 2)
            for p in (STEPS - 1, STEPS):
                sp.wait_ge(ring_dve, ring_position(STEPS, p, "ffn", 0)[2])
                store(p - 1)
            sp.wait_ge(out_stored, 32 * (STEPS + 1))

        @block.gpsimd
        def _(pool):
            nc.gpsimd.memset(ones[:], 1.0).then_inc(consts_ready, 1)
            nc.gpsimd.memset(xs[0][:], 0.0).then_inc(x_zeroed, 1)
            nc.gpsimd.memset(xs[1][:], 0.0).then_inc(x_zeroed, 1)
            nc.gpsimd.memset(ident[:], 0.0).then_inc(ident_zero, 1)
            nc.gpsimd.memset(minus_half[:], -0.5).then_inc(consts_ready, 1)
            nc.gpsimd.memset(eps[:], EPS).then_inc(consts_ready, 1)
            pool.wait_ge(ident_zero, 1)
            nc.gpsimd.affine_select(out=ident[:], in_=ident[:], compare_op=ALU.not_equal, fill=1.0, base=0,
                                    pattern=[[-1, 128]], channel_multiplier=1).then_inc(consts_ready, 1)
            pool.wait_ge(consts_ready, 3)

            def x_rstd(p):
                pool.wait_ge(xmv_ready, p + 1)
                nc.gpsimd.tensor_tensor(xvar[0:R, :], xmv[0:R, 1:2], eps[0:R, :], ALU.add).then_inc(xvar_ready, 1)
                pool.wait_ge(xvar_ready, p + 1)
                nc.gpsimd.tensor_tensor(xrstd[0:R, :], xvar[0:R, :], minus_half[0:R, :],
                                        ALU.pow).then_inc(xrstd_ready, 1)

            def y_rstd(p):
                pool.wait_ge(ymv_ready, p + 1)
                nc.gpsimd.tensor_tensor(yvar[0:R, :], ymv[0:R, 1:2], eps[0:R, :], ALU.add).then_inc(yvar_ready, 1)
                pool.wait_ge(yvar_ready, p + 1)
                nc.gpsimd.tensor_tensor(yrstd[0:R, :], yvar[0:R, :], minus_half[0:R, :],
                                        ALU.pow).then_inc(yrstd_ready, 1)

            x_rstd(0)
            x_rstd(1)
            def step(p, par):
                y_rstd(p - 1)
                x_rstd(p + 1)

            with pool.Fori(0, STEPS // 2 - 1) as i:
                step(i * 2 + 1, 1)
                step(i * 2 + 2, 0)
            y_rstd(STEPS - 2)
            y_rstd(STEPS - 1)

        def setup_bank(xc):
            return (ring[2], ring[3], ring[0], attended)[xc][:, :]

        def permuted(ap):
            return ap.rearrange("p (r c) -> p c r", c=C)

        def ring_take(engine, p, what, index):
            bank, n, _, _ = ring_position(STEPS, p, what, index)
            engine.wait_ge(ring_full, n)
            return ring[bank]

        @block.scalar
        def _(act):
            def copy(out_ap, in_ap):
                return nc.scalar.activation(out_ap, in_ap, ACT.Copy)

            def keys_evac(p, i):
                if ring_position(STEPS, p, "kT", i)[3] == "act":
                    bank = ring_take(act, p, "kT", i)
                    copy(keysT[:, i % 2, i // 2, :], bank[:, 0:GK]).then_inc(ring_act, 1)

            def x_evac(p):
                bank = ring_take(act, p, "xT", 0)
                copy(xnT[:, :, 0:R], bank[:, 0:C * R].rearrange("p (c r) -> p c r", c=C)).then_inc(ring_act, 1)

            def exps(p, g):
                if g == 0:
                    act.wait_ge(ebias_ready, p + 1)
                nc.scalar.activation(probs[0:R, KPG * g:KPG * (g + 1), :],
                                     scores[0:R, g, 0:GK].rearrange("r (k q) -> r k q", q=Q), ACT.Exp,
                                     bias=ebias[0:R, :], scale=1.0,
                                     accum_out=gsum[0:R, g:g + 1]).then_inc(exp_ready, 1)

            def probs_evac(p, g):
                bank = ring_take(act, p + 1, "pT", g)
                copy(probsT[0:Q, KPG * g:KPG * (g + 1), :],
                     bank[0:Q, 0:KPG * R].rearrange("q (k r) -> q k r", r=R)).then_inc(ring_act, 1)

            act.wait_ge(gabs_ready, 1)
            nc.scalar.activation(gexp[:], gabs[:], ACT.Exp, scale=-1.0).then_inc(gexp_ready, 1)
            act.wait_ge(gexp_ready, 1)
            nc.scalar.activation(glog[:], gexp[:], ACT.Ln, bias=1.0).then_inc(glog_ready, 1)
            for xc in (0, 2):
                act.wait_ge(setup_mm, xc + 1)
                nc.scalar.activation(wqk[:, xc, :].rearrange("p (c r) -> p c r", c=C),
                                     permuted(setup_bank(xc)), ACT.Copy, scale=SCALE).then_inc(setup_act, 1)

            def y_high(p):
                bank = ring_take(act, p + 1, "yT", 0)
                copy(x1nT_high[:, :, :], bank[:, 0:C * R].rearrange("p (c r) -> p c r", c=C)).then_inc(y_high_ready, 1)

            def step(p, par, half):
                first = isinstance(p, int) and p == 0
                x_evac(p)
                for i in range(8):
                    keys_evac(p, i)
                if not first:
                    probs_evac(p - 1, 0)
                    probs_evac(p - 1, 2)
                if first:
                    act.wait_ge(sign_loaded, 16)
                    copy(signs_high[:, :, :], signs).then_inc(signs_high_ready, 1)
                else:
                    y_high(p - 1)
                for g in range(GROUPS):
                    exps(p, g)

            over_steps(act, step)
            probs_evac(STEPS - 1, 0)
            probs_evac(STEPS - 1, 2)
            y_high(STEPS - 1)

        @block.vector
        def _(dve):
            def keys_evac(p, i):
                if ring_position(STEPS, p, "kT", i)[3] == "dve":
                    bank = ring_take(dve, p, "kT", i)
                    nc.vector.tensor_copy(keysT[:, i % 2, i // 2, :],
                                          bank[:, 0:GK]).then_inc(ring_dve, 1)

            def group_max(p, g):
                dve.wait_ge(scores_ready, p * GROUPS + ORDER.index(g) + 1)
                nc.vector.reduce_max(gmax[0:R, g:g + 1], scores[0:R, g, 0:GK], AX_X).then_inc(gmax_ready, 1)

            def softmax_bias(p):
                dve.wait_ge(gmax_ready, (p + 1) * GROUPS)
                nc.vector.reduce_max(smax[0:R, :], gmax[0:R, :], AX_X).then_inc(smax_ready, 1)
                dve.wait_ge(smax_ready, p + 1)
                dve.wait_ge(crow_ready, p + 1)
                nc.vector.tensor_tensor(cmax[0:R, :], smax[0:R, :], crow[0:R, :], ALU.add).then_inc(cmax_ready, 1)
                dve.wait_ge(cmax_ready, p + 1)
                nc.vector.tensor_tensor(ebias[0:R, :], crow[0:R, :], cmax[0:R, :],
                                        ALU.subtract).then_inc(ebias_ready, 1)

            def x_stats(p, par, half):
                dve.wait_ge(x_loaded[par], half * 32 + 32)
                nc.vector.bn_stats(xstat[0:R, :], xs[par][0:R, :]).then_inc(xstat_ready, 1)

            def x_aggregate(p):
                nc.vector.bn_aggr(xmv[0:R, :], xstat[0:R, :]).then_inc(xmv_ready, 1)

            def x_normalise(p, par):
                dve.wait_ge(xrstd_ready, p + 1)
                if not (isinstance(p, int) and p == 0):
                    dve.wait_ge(ring_full, ring_position(STEPS, p - 1, "xT", 0)[1])
                nc.vector.tensor_scalar(xn[0:R, :], xs[par][0:R, :], xmv[0:R, 0:1], xrstd[0:R, :],
                                        ALU.subtract, ALU.mult).then_inc(xn_ready, 1)

            def q_evac(p):
                bank = ring_take(dve, p, "q", 0)
                nc.vector.tensor_tensor(qT[:, :, :, :].rearrange("p c b t -> p c (b t)"),
                                        bank[:, 0:C * 2 * T].rearrange("p (c n) -> p c n", c=C),
                                        qbias[:, :].rearrange("p (c o) -> p c o", o=1).to_broadcast([128, C, 2 * T]),
                                        ALU.add).then_inc(ring_dve, 1)

            def c_column(p):
                nc.vector.tensor_tensor_reduce(out=cprod[0:R, :], in0=xn[0:R, :], in1=crep[0:R, :], scale=1.0,
                                               scalar=cconst[0:R, :], op0=ALU.mult, op1=ALU.add,
                                               accum_out=crow[0:R, :]).then_inc(crow_ready, 1)

            def side_transposes(p, unit, tiles=range(KPG)):
                g, b = 1 + unit // 2, unit % 2
                if tiles[0] == 0:
                    dve.wait_ge(side_loaded[b], p * 128 + (unit // 2 + 1) * 64)
                for k in tiles:
                    tr = nc.vector.transpose(sideT[g][:, b, :, k, :].rearrange("p c (r s) -> p s c r", s=4),
                                             side[b][:, :, k, :].rearrange("p s (a c) -> p s c a", c=C))
                if tiles[-1] == KPG - 1:
                    tr.then_inc(side_done, 1)

            def row_sums(p):
                dve.wait_ge(exp_ready, (p + 1) * GROUPS)
                nc.vector.reduce_sum(rsum[0:R, :], gsum[0:R, :], AX_X).then_inc(rsum_ready, 1)
                dve.wait_ge(rsum_ready, p + 1)
                nc.vector.reciprocal(rinv[0:R, :], rsum[0:R, :]).then_inc(rinv_ready, 1)

            def probs_evac(p, g):
                bank = ring_take(dve, p + 1, "pT", g)
                nc.vector.tensor_copy(probsT[0:Q, KPG * g:KPG * (g + 1), :],
                                      bank[0:Q, 0:KPG * R].rearrange("q (k r) -> q k r", r=R)).then_inc(ring_dve, 1)

            def residual(p, par):
                dve.wait_ge(attended_ready, p + 1)
                dve.wait_ge(rinv_ready, p + 1)
                nc.vector.scalar_tensor_tensor(out=x1[0:R, :], in0=attended[0:R, :], scalar=rinv[0:R, :],
                                               in1=xs[par][0:R, :], op0=ALU.mult, op1=ALU.add).then_inc(x1_ready, 1)

            def x1_stats(p):
                dve.wait_ge(x1_ready, p + 1)
                nc.vector.bn_stats(ystat[0:R, :], x1[0:R, :]).then_inc(ystat_ready, 1)

            def x1_aggregate(p):
                nc.vector.bn_aggr(ymv[0:R, :], ystat[0:R, :]).then_inc(ymv_ready, 1)

            def x1_normalise(p):
                dve.wait_ge(out_stored, p * 32 + 32)
                dve.wait_ge(yrstd_ready, p + 1)
                nc.vector.tensor_scalar(x1n[0:R, :], x1[0:R, :], ymv[0:R, 0:1], yrstd[0:R, :],
                                        ALU.subtract, ALU.mult).then_inc(x1n_ready, 1)

            def y_low(p):
                dve.wait_ge(y_high_ready, p + 1)
                bank = ring_take(dve, p + 1, "yT", 0)
                nc.vector.tensor_tensor(x1nT_low[:, :, :], bank[:, 0:C * R].rearrange("p (c r) -> p c r", c=C),
                                        x1nT_high[:, :, :].bitcast(F32), ALU.subtract).then_inc(ring_dve, 1)

            def finish(p):
                bank = ring_take(dve, p + 1, "ffn", 0)
                nc.vector.scalar_tensor_tensor(out=result[0:R, :], in0=bank[0:R, :], scalar=softplus[0:R, :],
                                               in1=x1[0:R, :], op0=ALU.mult, op1=ALU.add).then_inc(ring_dve, 1)

            def setup_product(xc):
                dve.wait_ge(setup_mm, xc + 1)
                nc.vector.tensor_scalar(wqk[:, xc, :].rearrange("p (c r) -> p c r", c=C),
                                        permuted(setup_bank(xc)), SCALE, None, ALU.mult).then_inc(setup_dve, 1)

            nc.vector.memset(scores[:, :, :], 0.0).then_inc(psum_zeroed, 1)
            nc.vector.memset(result[:], 0.0).then_inc(out_stored, 32)
            dve.wait_ge(b_loaded, 32)
            nc.vector.tensor_tensor(bprod[:], bqc[:], bkc[:], ALU.mult).then_inc(bprod_ready, 1)
            dve.wait_ge(consts_ready, 4)
            for dc in range(C):
                nc.vector.tensor_scalar(bkrep[:, dc, :], ones[:], bkc[:, dc:dc + 1], None,
                                        ALU.mult).then_inc(bkrep_ready, 1)
            dve.wait_ge(bprod_ready, 1)
            nc.vector.reduce_sum(bsum[:], bprod[:], AX_X).then_inc(bsum_ready, 1)
            x_stats(0, 0, 0)
            dve.wait_ge(xstat_ready, 1)
            x_aggregate(0)
            x_normalise(0, 0)
            side_transposes(0, 0)
            side_transposes(0, 1)
            dve.wait_ge(setup_small, 1)
            nc.vector.tensor_scalar(qbias[:], ring[0][:, 0:C], SCALE, None, ALU.mult).then_inc(smalls_copied, 1)
            nc.vector.tensor_scalar(cconst[:], ring[0][:, C:C + 1], SCALE, None, ALU.mult).then_inc(smalls_copied, 1)
            nc.vector.tensor_scalar(crep[:], ring[1][:, :], SCALE, None, ALU.mult).then_inc(smalls_copied, 1)
            nc.vector.tensor_copy(gain[:], ring[0][:, C + 1:C + 2]).then_inc(gain_copied, 1)
            dve.wait_ge(gain_copied, 1)
            nc.vector.scalar_tensor_tensor(out=gabs[:], in0=gain[:], scalar=-1.0, in1=gain[:],
                                           op0=ALU.mult, op1=ALU.max).then_inc(gabs_ready, 1)
            x_stats(1, 1, 0)
            dve.wait_ge(xstat_ready, 2)
            x_aggregate(1)
            dve.wait_ge(smalls_copied, 3)
            c_column(0)
            setup_product(1)
            dve.wait_ge(glog_ready, 1)
            nc.vector.scalar_tensor_tensor(out=softplus[:], in0=gain[:], scalar=0.0, in1=glog[:],
                                           op0=ALU.max, op1=ALU.add).then_inc(softplus_ready, 1)
            side_transposes(0, 2)
            setup_product(3)
            dve.wait_ge(setup_dve, 2)
            nc.vector.memset(attended[:, :], 0.0).then_inc(psum_zeroed, 1)
            dve.wait_ge(softplus_ready, 1)
            dve.wait_ge(psum_zeroed, 2)

            def step(p, par, half, last=False):
                first = isinstance(p, int) and p == 0
                for i in range(8):
                    keys_evac(p, i)
                q_evac(p)
                if first:
                    dve.wait_ge(crow_ready, 1)
                    side_transposes(p, 3)
                    dve.wait_ge(signs_high_ready, 1)
                    nc.vector.tensor_tensor(signs_low[:, :, :], signs, signs_high[:, :, :].bitcast(F32),
                                            ALU.subtract).then_inc(signs_split, 1)
                else:
                    row_sums(p - 1)
                    probs_evac(p - 1, 1)
                    c_column(p)
                    dve.wait_ge(crow_ready, p + 1)
                    dve.wait_ge(ring_full, ring_position(STEPS, p, "pT", 2)[1])
                    side_transposes(p, 2)
                    side_transposes(p, 3)
                    residual(p - 1, 1 - par)
                    x1_stats(p - 1)
                    dve.wait_ge(ystat_ready, p)
                group_max(p, 1)
                if not first:
                    x1_aggregate(p - 1)
                if not last:
                    side_transposes(p + 1, 0, range(2))
                if not first:
                    x1_normalise(p - 1)
                if not last:
                    side_transposes(p + 1, 0, range(2, KPG))
                if not (first or last):
                    x_stats(p + 1, 1 - par, half if par == 0 else half + 1)
                    dve.wait_ge(xstat_ready, p + 2)
                group_max(p, 2)
                if first:
                    x_normalise(1, 1)
                elif not last:
                    x_aggregate(p + 1)
                if not first:
                    y_low(p - 1)
                if not last:
                    side_transposes(p + 1, 1, range(KPG - 1))
                group_max(p, 0)
                softmax_bias(p)
                if not (first or last):
                    x_normalise(p + 1, 1 - par)
                if not last:
                    side_transposes(p + 1, 1, (KPG - 1,))
                if not first:
                    finish(p - 1)

            step(0, 0, 0)
            with dve.Fori(0, STEPS // 2 - 1) as i:
                step(i * 2 + 1, 1, i)
                step(i * 2 + 2, 0, i + 1)
            step(STEPS - 1, 1, STEPS // 2 - 1, last=True)
            p = STEPS - 1
            row_sums(p)
            probs_evac(p, 1)
            residual(p, 1)
            x1_stats(p)
            dve.wait_ge(ystat_ready, p + 1)
            x1_aggregate(p)
            x1_normalise(p)
            y_low(p)
            finish(p)

        @block.tensor
        def _(pe):
            def ring_bank(p, what, index):
                previous = ring_previous(STEPS, p, what, index)
                if previous:
                    pe.wait_ge(ring_sem[previous[0]], previous[1])
                return ring[ring_position(STEPS, p, what, index)[0]]

            def evacuated(p, what, index):
                _, _, n, engine = ring_position(STEPS, p, what, index)
                pe.wait_ge(ring_sem[engine], n)

            def transpose_x(p, src, ready, what):
                pe.wait_ge(ready[0], ready[1])
                bank = ring_bank(p, what, 0)
                for c in range(C):
                    mm = pe.transpose(bank[:, c * R:(c + 1) * R], src[0:R, c * 128:(c + 1) * 128], ident[0:R, 0:R])
                mm.then_inc(ring_full, 1)

            def transpose_keys(p, par, half, uses):
                pe.wait_ge(keys_loaded[par][0], half * 32 + 32)
                for i in uses:
                    b, c = i % 2, i // 2
                    bank = ring_bank(p, "kT", i)
                    for k in range(KPG):
                        mm = pe.transpose(bank[:, k * Q:(k + 1) * Q],
                                          permuted(keys[par][0:Q, b, k, :])[:, c], ident[0:Q, 0:Q])
                    mm.then_inc(ring_full, 1)

            xnT_b = xnT[:, :, :].rearrange("p c (b h) -> p c b h", b=2)

            def queries(p):
                bank = ring_bank(p, "q", 0)
                for yc in range(C):
                    for xc in range(C):
                        mm = pe.matmul(bank[:, yc * 2 * T:(yc + 1) * 2 * T], wqk[:, xc, yc * 128:(yc + 1) * 128],
                                       xnT_b[:, xc, :, 0:T], start=(xc == 0), stop=(xc == C - 1))
                mm.then_inc(ring_full, 1)

            def transpose_probs(p):
                for g in range(GROUPS):
                    pe.wait_ge(exp_ready, p * GROUPS + g + 1)
                    bank = ring_bank(p + 1, "pT", g)
                    for k in range(KPG):
                        mm = pe.transpose(bank[0:Q, k * R:(k + 1) * R], probs[0:R, KPG * g + k, :], ident[0:R, 0:R])
                    mm.then_inc(ring_full, 1)

            def attend(p, par, half):
                for g in (1, 2):
                    pe.wait_ge(keys_loaded[par][g], half * 32 + 32)
                for k in range(KT_N):
                    if k % KPG == 0:
                        evacuated(p + 1, "pT", k // KPG)
                    for b in range(2):
                        mm = pe.matmul(attended[b * HALF:b * HALF + T, :], probsT[0:Q, k, b * HALF:b * HALF + T],
                                       keys[par][0:Q, b, k, :], start=(k == 0), stop=(k == KT_N - 1))
                mm.then_inc(attended_ready, 1)

            def score(p, g):
                if g == ORDER[0]:
                    evacuated(p, "q", 0)
                    if not (isinstance(p, int) and p == 0):
                        pe.wait_ge(exp_ready, p * GROUPS)
                if g == 0:
                    evacuated(p, "kT", 7)
                else:
                    pe.wait_ge(side_done, p * UNITS + 2 * g)
                for c in range(C):
                    for b in range(2):
                        columns = sideT[g][:, b, c, :, PAD:] if g else keysT[:, b, c, :]
                        mm = pe.matmul(scores[b * HALF:b * HALF + T, g, 0:GK], qT[:, c, b, :], columns,
                                       start=(c == 0), stop=(c == C - 1))
                mm.then_inc(scores_ready, 1)

            def feed_forward(p):
                if isinstance(p, int) and p == 0:
                    pe.wait_ge(signs_split, 1)
                bank = ring_bank(p + 1, "ffn", 0)
                pe.wait_ge(y_high_ready, p + 1)
                for c in range(C):
                    pe.matmul(bank[0:R, :], x1nT_high[:, c, :], signs_high[:, c, :], start=(c == 0), stop=False)
                    pe.matmul(bank[0:R, :], x1nT_high[:, c, :], signs_low[:, c, :], start=False, stop=False)
                evacuated(p + 1, "yT", 0)
                for c in range(C):
                    mm = pe.matmul(bank[0:R, :], x1nT_low[:, c, :], signs_high[:, c, :], start=False, stop=(c == C - 1))
                mm.then_inc(ring_full, 1)

            def keep_warm(bank, times):
                for _ in range(times):
                    pe.matmul(bank[:, 0:128], ones[:, :], ones[:, :], start=True, stop=True)

            pe.wait_ge(consts_ready, 1)
            keep_warm(attended, 12)
            pe.wait_ge(wk_loaded, 16)
            pe.wait_ge(b_loaded, 32)
            for yc in range(C):
                for dc in range(C):
                    pe.matmul(ring[0][:, yc:yc + 1], permuted(wk[:, dc, :])[:, yc], bqc[:, dc:dc + 1],
                              start=(dc == 0), stop=(dc == C - 1))
            pe.wait_ge(wq_loaded, 16)
            pe.wait_ge(bkrep_ready, C)
            for dc in range(C):
                pe.matmul(ring[1][:, :], bkrep[:, dc, :], wq[:, dc, :], start=(dc == 0), stop=(dc == C - 1))
            pe.wait_ge(consts_ready, 4)
            pe.wait_ge(bsum_ready, 1)
            pe.matmul(ring[0][:, C:C + 1], ones[:, :], bsum[:, :], start=True, stop=True)
            pe.wait_ge(gain_loaded, 16)
            pe.matmul(ring[0][:, C + 1:C + 2], ones[0:1, :], gain_in[:, :], start=True,
                      stop=True).then_inc(setup_small, 1)
            for xc in range(C):
                if xc == 2:
                    pe.wait_ge(smalls_copied, 3)
                    pe.wait_ge(gain_copied, 1)
                for dc in range(C):
                    mm = pe.matmul(setup_bank(xc), wq[:, dc, xc * 128:(xc + 1) * 128], wk[:, dc, :],
                                   start=(dc == 0), stop=(dc == C - 1))
                mm.then_inc(setup_mm, 1)

            def step(p, par, half):
                first = isinstance(p, int) and p == 0
                if first:
                    pe.wait_ge(setup_act, 2)
                    pe.wait_ge(setup_dve, 1)
                transpose_x(p, xn, (xn_ready, p + 1), "xT")
                if first:
                    transpose_keys(p, par, half, range(6))
                    pe.wait_ge(setup_dve, 2)
                    queries(p)
                    transpose_keys(p, par, half, (6, 7))
                    pe.wait_ge(psum_zeroed, 2)
                else:
                    transpose_keys(p, par, half, range(8))
                    queries(p)
                    transpose_probs(p - 1)
                    attend(p - 1, 1 - par, half if par == 1 else half - 1)
                score(p, 1)
                score(p, 2)
                if not first:
                    transpose_x(p, x1n, (x1n_ready, p), "yT")
                score(p, 0)
                if not first:
                    feed_forward(p - 1)

            over_steps(pe, step)
            transpose_probs(STEPS - 1)
            attend(STEPS - 1, 1, STEPS // 2 - 1)
            keep_warm(scores[:, 0, :], 13)
            transpose_x(STEPS, x1n, (x1n_ready, STEPS), "yT")
            feed_forward(STEPS - 1)


_INS = ["x", "ctx_4096", "L0_xattn_Wq", "L0_xattn_bq", "L0_xattn_Wk", "L0_xattn_bk", "L0_ffn_sign", "L0_ffn_scale"]


def kernel(**inputs):
    import numpy as _np
    import concourse.bacc as _bacc
    from concourse import mybir as _mybir
    from concourse.bass_utils import run_bass_kernel_spmd as _run

    nc = _bacc.Bacc("TRN2", target_bir_lowering=False, num_devices=1)
    arrays, args = {}, []
    for name in _INS:
        a = _np.ascontiguousarray(inputs[name])
        if a.ndim == 0:
            a = a.reshape(1)
        arrays[f"in_{name}"] = a
        args.append(nc.dram_tensor(f"in_{name}", a.shape, _mybir.dt.from_np(a.dtype), kind="ExternalInput").ap())
    args.append(nc.dram_tensor("out_0", inputs["x"].shape, _mybir.dt.from_np(_np.dtype("float32")),
                               kind="ExternalOutput").ap())
    xattn_ffn_kernel(nc, *args)
    r = _run(nc, [arrays], core_ids=[0])
    return r.results[0]["out_0"]
```
